# Optimizing a Trainium2 kernel written in Bass

```python
import numpy as np
import jax
import jax.numpy as jnp

def _softmax(x, axis=-1):
    return jax.nn.softmax(x, axis=axis)

def _gelu(x):
    return jax.nn.gelu(x, approximate=True)

def _silu(x):
    return jax.nn.silu(x)

def _sigmoid(x):
    return jax.nn.sigmoid(x)

def _layernorm(x, axis=-1, eps=1e-05):
    m = jnp.mean(x, axis=axis, keepdims=True)
    v = jnp.var(x, axis=axis, keepdims=True)
    return (x - m) / jnp.sqrt(v + eps)

def _scatter_add(tgt, idx, src, axis=0):
    return tgt.at[idx].add(src)

def _segment_sum(src, seg, n):
    return jax.ops.segment_sum(src, seg, n)
kernel_name = 'mk_decoder_preln_d1_seqx_r2_537330'

def setup_inputs(seed: int=0):
    np.random.seed(seed)
    _w = jnp.asarray

    def _rec_inputs():
        import jax
        import jax.numpy as jnp
        _rk = jax.random.key(seed)
        x = 7.22e-05 + 1 * jax.random.normal(jax.random.fold_in(_rk, 1), (4, 1024, 1024), jnp.float32)
        _lenS = 1024 - jax.random.randint(jax.random.fold_in(_rk, 7), (4,), 0, max(1, 1024 // 4) + 1, jnp.int32)
        _lenS2 = 1024 - jax.random.randint(jax.random.fold_in(_rk, 8), (4,), 0, max(1, 1024 // 4) + 1, jnp.int32)
        _ctx_1024P = jax.random.normal(jax.random.fold_in(_rk, 11), (4, 16, 512), jnp.float32)
        _ctx_1024c = jax.random.dirichlet(jax.random.fold_in(_rk, 511), 0.3 * jnp.ones((16,), jnp.float32), (4, 1024))
        _ctx_1024t = jnp.einsum('bsk,bkd->bsd', _ctx_1024c, _ctx_1024P)
        _ctx_1024t = _ctx_1024t * jax.lax.rsqrt(jnp.mean(jnp.square(_ctx_1024t)) + 1e-12) * 0.953939
        ctx_1024 = 2.81802e-05 + 1.00001 * (_ctx_1024t + 0.3 * jax.random.normal(jax.random.fold_in(_rk, 611), (4, 1024, 512), jnp.float32))
        return (x, ctx_1024)
    x, ctx_1024 = _rec_inputs()

    def _L0_attn_setup():
        import jax, jax.numpy as jnp
        import numpy as np
        B, T, D, S = (8, 2048, 1024, 64)
        key = jax.random.key(seed)
        ks = jax.random.split(key, 7)
        sd_in = 1.0 / np.sqrt(D)
        sd_s = 1.0 / np.sqrt(S)
        x = jax.random.normal(ks[0], (B, T, D), jnp.float32)
        Wa = jax.random.uniform(ks[1], (S, D), jnp.float32, -sd_in, sd_in)
        ba = jax.random.uniform(ks[2], (S,), jnp.float32, -sd_in, sd_in)
        Wb = jax.random.uniform(ks[3], (S, D), jnp.float32, -sd_in, sd_in)
        bb = jax.random.uniform(ks[4], (S,), jnp.float32, -sd_in, sd_in)
        Wout = jax.random.uniform(ks[5], (D, S), jnp.float32, -sd_s, sd_s)
        bout = jax.random.uniform(ks[6], (D,), jnp.float32, -sd_s, sd_s)
        return {'x': x, 'Wa': Wa, 'ba': ba, 'Wb': Wb, 'bb': bb, 'Wout': Wout, 'bout': bout}
    _L0_attn_all = _L0_attn_setup()
    _L0_attn_in = {k: v for k, v in _L0_attn_all.items() if k in ('Wa', 'ba', 'Wb', 'bb', 'Wout', 'bout')}
    del _L0_attn_all

    def _L0_xattn_setup():
        import jax, jax.numpy as jnp
        import numpy as np
        key = jax.random.key(seed)
        ks = jax.random.split(key, 6)
        B, L, N, C, D = (8, 256, 1024, 512, 128)
        return {'teacher_logits': jax.random.normal(ks[0], (B, L, N), dtype=jnp.float32), 'teacher_features': jax.random.normal(ks[1], (B, N, C), dtype=jnp.float32), 'Wq': jax.random.normal(ks[2], (D, C), dtype=jnp.float32) * (1.0 / np.sqrt(C)), 'bq': jnp.zeros((D,), dtype=jnp.float32), 'Wk': jax.random.normal(ks[3], (D, C), dtype=jnp.float32) * (1.0 / np.sqrt(C)), 'bk': jnp.zeros((D,), dtype=jnp.float32)}
    _L0_xattn_all = _L0_xattn_setup()
    _L0_xattn_in = {k: v for k, v in _L0_xattn_all.items() if k in ('Wq', 'bq', 'Wk', 'bk')}
    del _L0_xattn_all

    def _L0_ffn_setup():
        import math
        import jax, jax.numpy as jnp
        import numpy as np
        DIM = 1024
        RANK = 8
        B, T = (4, 2048)

        def _orthogonal(key, n):
            a = jax.random.normal(key, (n, n), dtype=jnp.float32)
            q, r = jnp.linalg.qr(a)
            q = q * jnp.sign(jnp.diagonal(r))[None, :]
            return q
        key = jax.random.key(seed)
        kx, kf = jax.random.split(key)
        x = jax.random.normal(kx, (B, T, DIM), dtype=jnp.float32)
        fkeys = jax.random.split(kf, RANK)
        factors = jnp.stack([_orthogonal(fkeys[r], DIM) * (r + 1) ** (-0.5) for r in range(RANK)])
        bias = jnp.zeros((DIM,), dtype=jnp.float32)
        return {'x': x, 'factors': factors, 'bias': bias}
    _L0_ffn_all = _L0_ffn_setup()
    _L0_ffn_in = {k: v for k, v in _L0_ffn_all.items() if k in ('factors', 'bias')}
    del _L0_ffn_all
    return {'x': x, 'ctx_1024': ctx_1024, 'L0_attn_Wa': _L0_attn_in['Wa'], 'L0_attn_ba': _L0_attn_in['ba'], 'L0_attn_Wb': _L0_attn_in['Wb'], 'L0_attn_bb': _L0_attn_in['bb'], 'L0_attn_Wout': _L0_attn_in['Wout'], 'L0_attn_bout': _L0_attn_in['bout'], 'L0_xattn_Wq': _L0_xattn_in['Wq'], 'L0_xattn_bq': _L0_xattn_in['bq'], 'L0_xattn_Wk': _L0_xattn_in['Wk'], 'L0_xattn_bk': _L0_xattn_in['bk'], 'L0_ffn_factors': _L0_ffn_in['factors'], 'L0_ffn_bias': _L0_ffn_in['bias']}

def reference(x, ctx_1024, L0_attn_Wa, L0_attn_ba, L0_attn_Wb, L0_attn_bb, L0_attn_Wout, L0_attn_bout, L0_xattn_Wq, L0_xattn_bq, L0_xattn_Wk, L0_xattn_bk, L0_ffn_factors, L0_ffn_bias):
    import jax
    import jax.numpy as jnp

    def _L0_attn_ref(x, Wa, ba, Wb, bb, Wout, bout):
        import jax, jax.numpy as jnp
        import numpy as np
        B, T, D, S = (8, 2048, 1024, 64)
        a = jnp.tanh(jnp.einsum('btd,sd->bts', x, Wa) + ba)
        b = jnp.tanh(jnp.einsum('btd,sd->bts', x, Wb) + bb)

        def step(h, ab):
            at, bt = ab
            h = at * h + bt
            return (h, h)
        h0 = jnp.zeros((x.shape[0], Wa.shape[0]), x.dtype)
        _, hs = jax.lax.scan(step, h0, (jnp.swapaxes(a, 0, 1), jnp.swapaxes(b, 0, 1)))
        hs = jnp.swapaxes(hs, 0, 1)
        return x + jnp.einsum('bts,ds->btd', hs, Wout) + bout

    def _L0_xattn_ref(teacher_logits, teacher_features, Wq, bq, Wk, bk):
        import jax, jax.numpy as jnp
        import numpy as np
        query = jnp.einsum('bnc,dc->bnd', teacher_features, Wq) + bq
        key = jnp.einsum('bnc,dc->bnd', teacher_features, Wk) + bk
        energy = jnp.einsum('bnd,bmd->bnm', query, key)
        attention = jax.nn.softmax(energy, axis=-1)
        x_m = jnp.einsum('bln,bmn->blm', teacher_logits, attention)
        return x_m

    def _L0_ffn_ref(x, factors, bias):
        import math
        import jax, jax.numpy as jnp
        import numpy as np
        DIM = 1024
        RANK = 8
        B, T = (4, 2048)

        def _orthogonal(key, n):
            a = jax.random.normal(key, (n, n), dtype=jnp.float32)
            q, r = jnp.linalg.qr(a)
            q = q * jnp.sign(jnp.diagonal(r))[None, :]
            return q
        rank = factors.shape[0]
        mixed = jnp.einsum('btd,rde->bte', x, factors)
        mixed = mixed / math.sqrt(rank) + bias
        return mixed
    x = x + _L0_attn_ref(_layernorm(x, axis=-1), L0_attn_Wa, L0_attn_ba, L0_attn_Wb, L0_attn_bb, L0_attn_Wout, L0_attn_bout)
    x = x + _L0_xattn_ref(_layernorm(x, axis=-1), ctx_1024, L0_xattn_Wq, L0_xattn_bq, L0_xattn_Wk, L0_xattn_bk)
    x = x + _L0_ffn_ref(_layernorm(x, axis=-1), L0_ffn_factors, L0_ffn_bias)
    return x

_drawn_inputs = setup_inputs


def setup_inputs(seed=0):
    import zlib

    import numpy as np

    out = dict(_drawn_inputs(seed))
    spreads = {'L0_xattn_bq': (0.0, 0.1), 'L0_xattn_bk': (0.0, 2.0), 'L0_ffn_bias': (0.0, 0.1)}
    factors = {'L0_attn_ba': 22.173, 'L0_attn_bb': 8.0}
    for name, (base, spread) in spreads.items():
        noise = np.random.default_rng([zlib.crc32(name.encode()), seed]).standard_normal(out[name].shape)
        drawn = base * np.exp(spread * noise) if base else spread * noise
        out[name] = jnp.asarray(drawn.astype(out[name].dtype))
    for name, factor in factors.items():
        out[name] = (out[name] * factor).astype(out[name].dtype)
    return out
```

```python
from contextlib import ExitStack

import concourse.bass as bass
from concourse import mybir

ALU = mybir.AluOpType
ACT = mybir.ActivationFunctionType
AX = mybir.AxisListType
F32 = mybir.dt.float32
F16 = mybir.dt.float16
I32 = mybir.dt.int32

P = 128
HALF = 512
EPS = 1e-5
XN_SCALE = 2.0 ** 10
PROB_SCALE = 2.0 ** 15
HS_SCALE = 2.0 ** 4
W_TOP = 2.0 ** 14

LEAD = dict(ctx=17, energy=9, probs=8, ln1=2, mixer=1, attend=0, ffn=-1)
LOADS = dict(ctx_load=19, x_load=3, store=-1)


class Tile:

    def __init__(self, half, odd, first):
        self.half, self.odd, self.first = half, odd, first

    @property
    def n(self):
        return 2 * self.half + self.odd


class Slice:

    def __init__(self, half, odd, first):
        self.half, self.odd, self.first = half, odd, first

    def tile(self, lead, tiles, start=0):
        first = self.first + lead
        if not start <= first < tiles:
            return None
        odd = (self.odd + lead) % 2
        return Tile(self.half + (self.odd + lead - odd) // 2, odd, first)


def walk(eng, leads, tiles, body, starts=None, cuts=()):
    starts = starts or {}
    lo = min(starts.get(k, 0) - v for k, v in leads.items())
    hi = max(tiles - v for v in leads.values())

    def active(s):
        def state(k, v):
            t, t0 = s + v, starts.get(k, 0)
            return 0 if t < t0 or t >= tiles else (1 + t - t0 if t - t0 < 2 else 3)
        return tuple(state(k, v) for k, v in sorted(leads.items())) + tuple(s >= c for c in cuts)

    s = lo
    while s < hi:
        e = s
        while e < hi and active(e) == active(s):
            e += 1
        pairs = (e - s) // 2
        if pairs >= 2:
            c, odd = s // 2, s % 2
            with eng.Fori(0, pairs) as i:
                body(Slice(i + c, odd, s))
                body(Slice(i + c + odd, 1 - odd, s + 1))
            s += 2 * pairs
        else:
            body(Slice(s // 2, s % 2, s))
            s += 1


def decoder_kernel(nc, x, ctx_in, wa, ba, wb, bb, wout, bout, wq, bq, wk, bk, factors, fbias, out):
    B, T, D = x.shape
    C = ctx_in.shape[2]
    S = wa.shape[0]
    R = factors.shape[0]
    TILES = B * T // P
    PER = T // P
    KD, KC = D // P, C // P
    assert 2 * S == P and wq.shape[0] == P and T == D == 2 * HALF and ctx_in.shape[1] == T and PER == 8
    RSQRT_R = float(R) ** -0.5

    x_rows = x.rearrange("b (j p) d -> (b j) p d", p=P)
    ctx_rows = ctx_in.rearrange("b (j p) c -> (b j) p c", p=P)
    out_rows = out.rearrange("b (j p) d -> (b j) p d", p=P)
    f_rows = factors.rearrange("r (k p) e -> r p k e", p=P)

    with ExitStack() as stack:
        def sb(name, shape, dt=F32):
            return stack.enter_context(nc.sbuf_tensor(name, shape, dt))

        def sem(name):
            return stack.enter_context(nc.semaphore(name))

        def psum(name):
            return stack.enter_context(nc.psum_tensor(name, [P, 2 * HALF], F32))

        ps_attend, ps_ffn, ps_c, ps_t = psum("ps_attend"), psum("ps_ffn"), psum("ps_c"), psum("ps_t")

        pt_hi = sb("pt_hi", [P, 2, KD, T], F16)
        pt_lo = sb("pt_lo", [P, 2, KD, T], F16)
        f_store = sb("f_store", [P, KD + 1, D])
        x_in = sb("x_in", [P, 2, D])
        x_mid = sb("x_mid", [P, 2, D])
        x_out = sb("x_out", [P, 2, D])
        xn1, xn2, xn3 = sb("xn1", [P, D]), sb("xn2", [P, D]), sb("xn3", [P, D])
        xn1T = sb("xn1T", [P, 2, D], F16)
        xn2T = sb("xn2T", [P, 2, D], F16)
        xn3T = sb("xn3T", [P, 2, 2, D], F16)
        ctx_nat = sb("ctx_nat", [P, 2, C])
        ctxT = sb("ctxT", [P, C])
        qT = sb("qT", [P, 2, T])
        kT = sb("kT", [P, 2, T])
        q_tile = sb("q_tile", [P, P])
        probs = sb("probs", [P, T])
        wabT = sb("wabT", [P, 2, D], F16)
        woutT = sb("woutT", [P, 2, D], F16)
        wqT = sb("wqT", [P, C])
        wkT = sb("wkT", [P, C])
        wab_nat, wout_nat = x_mid[:, 0, :], x_mid[:, 1, :]
        wq_nat, wk_nat = x_out[:, 0, 0:C], x_out[:, 0, C:2 * C]
        bout_all = sb("bout_all", [P, D])
        fbias_all = sb("fbias_all", [P, D])
        ident = sb("ident", [P, P])
        bq_col, bk_col = sb("bq_col", [P, 1]), sb("bk_col", [P, 1])
        bab_col = sb("bab_col", [P, 1])
        gate_a = sb("gate_a", [S, P])
        gate_b = sb("gate_b", [S, P])
        hs = sb("hs", [S, P])
        hs_parts = sb("hs_parts", [P, P], F16)
        carry = sb("carry", [S, 1])
        keep = sb("keep", [S, TILES + 1])
        stats = sb("stats", [P, 3, 12])
        meanvar = sb("meanvar", [P, 3, 2])
        norm = sb("norm", [P, 3, 4])
        affine = sb("affine", [P, 2])
        minus_half = sb("minus_half", [P, 1])
        neg_max = sb("neg_max", [P, 1])
        row_sum = sb("row_sum", [P, 1])
        row_inv = sb("row_inv", [P, 1])
        wab_s, wout_s, f_s = sb("wab_s", [P, 6]), sb("wout_s", [P, 6]), sb("f_s", [P, 6])

        wqk_loaded, wab_loaded, wout_loaded = sem("wqk_loaded"), sem("wab_loaded"), sem("wout_loaded")
        cols_loaded, rows_loaded = sem("cols_loaded"), sem("rows_loaded")
        f_loaded = sem("f_loaded")
        x_loaded = [sem("x_loaded0"), sem("x_loaded1")]
        ctx_loaded = [sem("ctx_loaded0"), sem("ctx_loaded1")]
        stored = [sem("stored0"), sem("stored1")]
        ident_ready, const_ready, gp_const_ready = sem("ident_ready"), sem("const_ready"), sem("gp_const_ready")
        w_psum, w_psum_read = sem("w_psum"), sem("w_psum_read")
        wab_step, wout_step, f_step = sem("wab_step"), sem("wout_step"), sem("f_step")
        w_rowmax, w_allmax, w_scaled, w_hi = (
            sem("w_rowmax"), sem("w_allmax"), sem("w_scaled"), sem("w_hi"))
        f_max, f_allmax, f_hi, f_lo = sem("f_max"), sem("f_allmax"), sem("f_hi"), sem("f_lo")
        wait_carrier = sem("wait_carrier")
        ctx_turned, ctxT_ready, qk_done, qk_ready = (
            sem("ctx_turned"), sem("ctxT_ready"), sem("qk_done"), sem("qk_ready"))
        q_tile_ready, energy_done, max_ready, exp_done, inv_ready, probs_ready = (
            sem("q_tile_ready"), sem("energy_done"), sem("max_ready"), sem("exp_done"), sem("inv_ready"),
            sem("probs_ready"))
        probs_turned, pt_hi_ready, pt_ready = sem("probs_turned"), sem("pt_hi_ready"), sem("pt_ready")
        ln_parts = [sem(f"ln{k}_parts") for k in range(3)]
        ln_stats = [sem(f"ln{k}_stats") for k in range(3)]
        ln_var = [sem(f"ln{k}_var") for k in range(3)]
        ln_rstd = [sem(f"ln{k}_rstd") for k in range(3)]
        ln_scales = [sem(f"ln{k}_scales") for k in range(3)]
        ln_done = [sem(f"ln{k}_done") for k in range(3)]
        xn_turned = [sem(f"xn{k}_turned") for k in range(3)]
        xn_hi = [sem(f"xn{k}_hi") for k in range(3)]
        xnT_ready = [sem(f"xn{k}T_ready") for k in range(3)]
        affine_done, res1_ready = sem("affine_done"), sem("res1_ready")
        ab_done, gates_ready, scan_done, hs_hi, hs_ready, carry_ready = (
            sem("ab_done"), sem("gates_ready"), sem("scan_done"), sem("hs_hi"), sem("hs_ready"), sem("carry_ready"))
        mixer_done, x1_ready = sem("mixer_done"), sem("x1_ready")
        attend_done, x2_ready, bias_added, ffn_done, out_ready = (
            sem("attend_done"), sem("x2_ready"), sem("bias_added"), sem("ffn_done"), sem("out_ready"))

        blocks8 = lambda ap: ap.rearrange("p (k m) -> p k m", m=P)
        wout_4d = wout_nat.rearrange("p (k a s) -> p k a s", k=KD, a=2)
        f_part = lambda k: f_store[:, k + 1, :].bitcast(F16)
        xns = (xn1, xn2, xn3)

        def parity(t):
            return (t.half // (PER // 2)) % 2

        def in_batch(t):
            return (t.half % (PER // 2)) * (2 * P) + t.odd * P

        def batch_tiles(t):
            return (t.half // (PER // 2)) * PER + PER

        block = stack.enter_context(nc.Block())

        @block.sync
        def _(sp):
            sp.dma_start(wq_nat, wq).then_inc(wqk_loaded, 16)
            sp.dma_start(wk_nat, wk).then_inc(wqk_loaded, 16)
            for t in range(2):
                sp.dma_start(ctx_nat[:, t, :], ctx_rows[t]).then_inc(ctx_loaded[t], 16)
            with nc.allow_non_contiguous_dma(reason="bias columns, 128 words each"):
                sp.dma_start(bq_col[:, :], bq.rearrange("(p a) -> p a", a=1)).then_inc(cols_loaded, 16)
                sp.dma_start(bk_col[:, :], bk.rearrange("(p a) -> p a", a=1)).then_inc(cols_loaded, 16)
                sp.dma_start(bab_col[0:S, :], ba.rearrange("(p a) -> p a", a=1)).then_inc(cols_loaded, 16)
                sp.dma_start(bab_col[S:P, :], bb.rearrange("(p a) -> p a", a=1)).then_inc(cols_loaded, 16)
            sp.dma_start(wab_nat[0:S, :], wa).then_inc(wab_loaded, 16)
            sp.dma_start(wab_nat[S:P, :], wb).then_inc(wab_loaded, 16)
            for copy in range(2):
                sp.dma_start(wout_4d[:, :, copy, :], wout.rearrange("(k p) s -> p k s", p=P)).then_inc(wout_loaded, 16)
            for t in range(2):
                sp.dma_start(x_in[:, t, :], x_rows[t]).then_inc(x_loaded[t], 16)
            sp.dma_start(bout_all[:, :], bout.partition_broadcast(P)).then_inc(rows_loaded, 16)
            sp.dma_start(fbias_all[:, :], fbias.partition_broadcast(P)).then_inc(rows_loaded, 16)

            def loads(sl):
                t = sl.tile(LOADS["ctx_load"], TILES, 2)
                if t:
                    sp.wait_ge(ctx_turned, t.n - 1)
                    sp.dma_start(ctx_nat[:, t.odd, :], ctx_rows[t.n]).then_inc(ctx_loaded[t.odd], 16)
                t = sl.tile(LOADS["x_load"], TILES, 2)
                if t:
                    sp.wait_ge(x1_ready, t.n - 1)
                    sp.dma_start(x_in[:, t.odd, :], x_rows[t.n]).then_inc(x_loaded[t.odd], 16)
                t = sl.tile(LOADS["store"], TILES)
                if t:
                    sp.wait_ge(out_ready, t.n + 1)
                    sp.dma_start(out_rows[t.n], x_out[:, t.odd, :]).then_inc(stored[t.odd], 16)

            walk(sp, LOADS, TILES, loads, starts=dict(ctx_load=2, x_load=2))
            for odd in range(2):
                sp.wait_ge(stored[odd], 16 * TILES // 2)

        @block.gpsimd
        def _(gp):
            for r in range(R):
                if r:
                    gp.wait_ge(f_loaded, 16 * r)
                    gp.dma_start(f_store[:, 0:KD, :], f_rows[r], accum_op=ALU.add).then_inc(f_loaded, 16)
                else:
                    gp.dma_start(f_store[:, 0:KD, :], f_rows[r]).then_inc(f_loaded, 16)
                    gp.memset(ident[:, :], 0.0).then_inc(gp_const_ready, 1)
                    gp.memset(minus_half[:, :], -0.5).then_inc(gp_const_ready, 1)
                    gp.wait_ge(gp_const_ready, 2)
                    gp.affine_select(out=ident[:, :], in_=ident[:, :], compare_op=ALU.not_equal, fill=1.0, base=0,
                                     pattern=[[-1, P]], channel_multiplier=1).then_inc(ident_ready, 1)
                    gp.wait_ge(w_rowmax, 2)
                    gp.partition_all_reduce(wout_s[:, 1:2], wout_s[:, 0:1], P, bass.bass_isa.ReduceOp.max)\
                      .then_inc(w_allmax, 1)

            def carry_wait():
                gp.sem_inc(wait_carrier, 1)

            def scales(k, t):
                gp.wait_ge(ln_stats[k], t.n + 1)
                if t.first:
                    gp.wait_ge(ln_done[k], t.n)
                carry_wait()
                gp.tensor_scalar(norm[:, k, 0:1], meanvar[:, k, 1:2], EPS, XN_SCALE ** -2, ALU.add, ALU.mult)\
                  .then_inc(ln_var[k], 1)
                gp.wait_ge(ln_var[k], t.n + 1)
                gp.tensor_tensor(norm[:, k, 1:2], norm[:, k, 0:1], minus_half[:, :], ALU.pow).then_inc(ln_rstd[k], 1)
                gp.wait_ge(ln_rstd[k], t.n + 1)
                carry_wait()
                gp.tensor_scalar(norm[:, k, 2:3], meanvar[:, k, 0:1], norm[:, k, 1:2], -1.0, ALU.mult, ALU.mult)\
                  .then_inc(ln_scales[k], 1)

            def body(sl):
                t = sl.tile(LEAD["mixer"], TILES)
                if t:
                    gp.wait_ge(ln_done[0], t.n + 1)
                    carry_wait()
                    gp.tensor_scalar(affine[:, 0:1], norm[:, 0, 1:2], 1.0 / XN_SCALE, 1.0, ALU.mult, ALU.add)
                    gp.tensor_scalar(affine[:, 1:2], norm[:, 0, 2:3], 1.0 / XN_SCALE, 0.0, ALU.mult, ALU.add)\
                      .then_inc(affine_done, 1)
                    gp.wait_ge(affine_done, 2 * t.n + 1)
                    carry_wait()
                    gp.tensor_scalar(x_in[:, t.odd, :], x_in[:, t.odd, :], affine[:, 0:1], affine[:, 1:2],
                                     ALU.mult, ALU.add).then_inc(affine_done, 1)
                    if t.first == 0:
                        gp.wait_ge(rows_loaded, 32)
                    gp.wait_ge(affine_done, 2 * t.n + 2)
                    gp.tensor_tensor(x_in[:, t.odd, :], x_in[:, t.odd, :], bout_all[:, :], ALU.add)\
                      .then_inc(res1_ready, 1)
                t = sl.tile(LEAD["probs"], TILES)
                if t:
                    gp.wait_ge(inv_ready, t.n + 1)
                    carry_wait()
                    gp.tensor_scalar(probs[:, :], probs[:, :], row_inv[:, :], PROB_SCALE, ALU.mult, ALU.mult)\
                      .then_inc(probs_ready, 1)
                t = sl.tile(LEAD["energy"], TILES)
                if t:
                    gp.wait_ge(qk_ready, 2 * t.n + 2)
                    if t.first:
                        gp.wait_ge(energy_done, t.n)
                    gp.tensor_copy(q_tile[:, :], qT[:, parity(t), bass.ds(in_batch(t), P)]).then_inc(q_tile_ready, 1)
                t = sl.tile(LEAD["attend"], TILES)
                if t:
                    scales(2, t)
                    gp.wait_ge(x2_ready, t.n + 1)
                    if t.first >= 2:
                        gp.wait_ge(stored[t.odd], 16 * t.half)
                    gp.tensor_tensor(x_out[:, t.odd, :], x_mid[:, t.odd, :], fbias_all[:, :], ALU.add)\
                      .then_inc(bias_added, 1)
                    if t.first == 0:
                        gp.wait_ge(f_max, 1)
                        gp.partition_all_reduce(f_s[:, 1:2], f_s[:, 0:1], P, bass.bass_isa.ReduceOp.max)\
                          .then_inc(f_allmax, 1)
                t = sl.tile(LEAD["mixer"], TILES)
                if t:
                    scales(1, t)
                t = sl.tile(LEAD["ln1"], TILES)
                if t:
                    scales(0, t)

            walk(gp, LEAD, TILES, body)

        @block.scalar
        def _(act):
            def high(out_ap, psum_ap, scale=1.0):
                return nc.scalar.activation(out_ap, psum_ap, ACT.Copy, scale=scale)

            act.wait_ge(w_psum, 1)
            nc.scalar.copy(wqT[:, :], ps_t[:, 0:C]).then_inc(w_psum_read, 1)
            nc.scalar.copy(wkT[:, :], ps_t[:, C:2 * C]).then_inc(w_psum_read, 1)
            act.wait_ge(w_psum, 2)
            high(wabT[:, 0, :], ps_c[:, :]).then_inc(w_hi, 1)
            act.wait_ge(w_psum, 3)
            high(woutT[:, 0, :], ps_attend[:, :]).then_inc(w_hi, 1)

            def normalise(k, t, src):
                act.wait_ge(ln_scales[k], t.n + 1)
                if t.first:
                    act.wait_ge(xn_turned[k], t.n)
                nc.scalar.activation(xns[k][:, :], src, ACT.Identity, bias=norm[:, k, 2:3], scale=norm[:, k, 1:2])\
                  .then_inc(ln_done[k], 1)

            def body(sl):
                t = sl.tile(LEAD["mixer"], TILES)
                if t:
                    act.wait_ge(xn_turned[0], t.n + 1)
                    if t.first:
                        act.wait_ge(ab_done, t.n)
                    high(xn1T[:, 0, :], ps_t[:, :]).then_inc(xn_hi[0], 1)
                    act.wait_ge(ab_done, t.n + 1)
                    if t.first == 0:
                        act.wait_ge(cols_loaded, 64)
                    if t.first:
                        act.wait_ge(scan_done, t.n)
                    nc.scalar.activation(gate_a[:, :], ps_t[0:S, 0:P], ACT.Tanh, bias=bab_col[0:S, :],
                                         scale=wab_s[0:S, 4:5])
                    nc.scalar.activation(gate_b[:, :], ps_t[S:P, 0:P], ACT.Tanh, bias=bab_col[S:P, :],
                                         scale=wab_s[S:P, 4:5]).then_inc(gates_ready, 1)
                t = sl.tile(LEAD["ctx"], TILES)
                if t:
                    act.wait_ge(ctx_turned, t.n + 1)
                    if t.first:
                        act.wait_ge(qk_done, t.n)
                    nc.scalar.copy(ctxT[:, :], ps_t[:, HALF:HALF + C]).then_inc(ctxT_ready, 1)
                t = sl.tile(LEAD["attend"], TILES)
                if t:
                    normalise(2, t, x_mid[:, t.odd, :])
                    if t.first == 0:
                        act.wait_ge(f_step, 4)
                        for n, k in enumerate(reversed(range(KD))):
                            if n:
                                act.wait_ge(f_lo, n)
                            nc.scalar.activation(f_part(k)[:, 0:D], f_store[:, k, :], ACT.Copy, scale=f_s[:, 3:4])\
                              .then_inc(f_hi, 1)
                t = sl.tile(LEAD["ctx"], TILES)
                if t:
                    act.wait_ge(qk_done, t.n + 1)
                    if t.first == 0:
                        act.wait_ge(cols_loaded, 64)
                    if t.first > PER:
                        act.wait_ge(energy_done, t.n - PER)
                    for dst, at, bias in ((qT, 0, bq_col), (kT, P, bk_col)):
                        nc.scalar.activation(dst[:, parity(t), bass.ds(in_batch(t), P)], ps_t[:, at:at + P],
                                             ACT.Identity, bias=bias[:, :]).then_inc(qk_ready, 1)
                t = sl.tile(LEAD["mixer"], TILES)
                if t:
                    normalise(1, t, x_mid[:, t.odd, :])
                t = sl.tile(LEAD["attend"], TILES)
                if t:
                    act.wait_ge(xn_turned[2], t.n + 1)
                    if t.first >= 2:
                        act.wait_ge(ffn_done, t.n - 1)
                    high(xn3T[:, t.odd, 0, :], ps_t[:, :]).then_inc(xn_hi[2], 1)
                t = sl.tile(LEAD["probs"], TILES)
                if t:
                    act.wait_ge(probs_turned, t.n + 1)
                    if t.first > PER:
                        act.wait_ge(attend_done, t.n - PER)
                    high(pt_hi[:, parity(t), :, bass.ds(in_batch(t), P)], blocks8(ps_c[:, :])).then_inc(pt_hi_ready, 1)
                t = sl.tile(LEAD["mixer"], TILES)
                if t:
                    act.wait_ge(xn_turned[1], t.n + 1)
                    if t.first:
                        act.wait_ge(attend_done, t.n)
                    high(xn2T[:, 0, :], ps_t[:, :]).then_inc(xn_hi[1], 1)
                t = sl.tile(LEAD["energy"], TILES)
                if t:
                    act.wait_ge(max_ready, t.n + 1)
                    if t.first:
                        act.wait_ge(probs_turned, t.n)
                        act.wait_ge(inv_ready, t.n)
                    nc.scalar.activation(probs[:, :], ps_c[:, :], ACT.Exp, bias=neg_max[:, :],
                                         accum_out=row_sum[:, :]).then_inc(exp_done, 1)
                t = sl.tile(LEAD["ln1"], TILES)
                if t:
                    normalise(0, t, x_in[:, t.odd, :])

            walk(act, LEAD, TILES, body)

        @block.vector
        def _(dve):
            V = nc.vector
            V.memset(keep[:, :], 1.0).then_inc(const_ready, 1)
            dve.wait_ge(const_ready, 1)
            V.memset(keep[:, 0:TILES + 1:PER], 0.0)
            V.memset(carry[:, :], 0.0).then_inc(const_ready, 1)

            def power_scale(s, src, carried, step):
                V.tensor_scalar(s[:, 2:3], s[:, src:src + 1], 1e-30, None, ALU.max).then_inc(step, 1)
                dve.wait_ge(step, 1)
                V.tensor_scalar(s[:, 5:6].bitcast(I32), s[:, 2:3].bitcast(I32), 0x7F800000, None, ALU.bitwise_and)\
                 .then_inc(step, 1)
                dve.wait_ge(step, 2)
                V.tensor_scalar(s[:, 4:5], s[:, 5:6], carried / W_TOP, None, ALU.mult)
                V.tensor_scalar(s[:, 2:3], s[:, 5:6], 1.0 / W_TOP, None, ALU.mult).then_inc(step, 1)
                dve.wait_ge(step, 3)
                V.reciprocal(s[:, 3:4], s[:, 2:3]).then_inc(step, 1)
                dve.wait_ge(step, 4)

            dve.wait_ge(wab_loaded, 32)
            V.tensor_reduce(wab_s[:, 0:1], wab_nat, AX.X, ALU.max, apply_absolute_value=True)\
             .then_inc(w_rowmax, 1)
            dve.wait_ge(wout_loaded, 32)
            V.tensor_reduce(wout_s[:, 0:1], wout_nat, AX.X, ALU.max, apply_absolute_value=True)\
             .then_inc(w_rowmax, 1)
            dve.wait_ge(w_rowmax, 1)
            power_scale(wab_s, 0, 1.0 / XN_SCALE, wab_step)
            V.tensor_scalar(wab_nat, wab_nat, wab_s[:, 3:4], None, ALU.mult).then_inc(w_scaled, 1)
            dve.wait_ge(w_allmax, 1)
            power_scale(wout_s, 1, 1.0 / HS_SCALE, wout_step)
            V.tensor_scalar(wout_nat, wout_nat, wout_s[:, 3:4], None, ALU.mult).then_inc(w_scaled, 1)
            dve.wait_ge(w_hi, 1)
            V.tensor_tensor(wabT[:, 1, :], ps_c[:, :], wabT[:, 0, :], ALU.subtract).then_inc(w_psum_read, 1)
            dve.wait_ge(w_hi, 2)
            V.tensor_tensor(woutT[:, 1, :], ps_attend[:, :], woutT[:, 0, :], ALU.subtract).then_inc(w_psum_read, 1)

            def low(out_ap, psum_ap, high_ap):
                return V.tensor_tensor(out_ap, psum_ap, high_ap, ALU.subtract)

            def moments(k, t, src):
                if t.first:
                    dve.wait_ge(ln_scales[k], t.n)
                for h in range(2):
                    V.bn_stats(stats[:, k, 6 * h:6 * h + 6], src[:, h * HALF:(h + 1) * HALF]).then_inc(ln_parts[k], 1)
                dve.wait_ge(ln_parts[k], 2 * t.n + 2)
                dve.sem_inc(wait_carrier, 1)
                V.bn_aggr(meanvar[:, k, :], stats[:, k, :]).then_inc(ln_stats[k], 1)

            def body(sl):
                t = sl.tile(LEAD["probs"], TILES)
                if t:
                    dve.wait_ge(exp_done, t.n + 1)
                    if t.first:
                        dve.wait_ge(probs_ready, t.n)
                    V.reciprocal(row_inv[:, :], row_sum[:, :]).then_inc(inv_ready, 1)
                t = sl.tile(LEAD["mixer"], TILES)
                if t:
                    dve.wait_ge(xn_hi[0], t.n + 1)
                    low(xn1T[:, 1, :], ps_t[:, :], xn1T[:, 0, :]).then_inc(xnT_ready[0], 1)
                t = sl.tile(LEAD["attend"], TILES)
                if t:
                    dve.wait_ge(attend_done, t.n + 1)
                    mid = x_mid[:, t.odd, :]
                    V.scalar_tensor_tensor(mid, ps_attend[:, :], 1.0 / (XN_SCALE * PROB_SCALE), mid, ALU.mult, ALU.add)\
                     .then_inc(x2_ready, 1)
                    dve.wait_ge(x2_ready, t.n + 1)
                    moments(2, t, mid)
                    if t.first == 0:
                        dve.wait_ge(f_loaded, 16 * R)
                        V.tensor_reduce(f_s[:, 0:1], f_store[:, 0:KD, :], AX.XY, ALU.max, apply_absolute_value=True)\
                         .then_inc(f_max, 1)
                t = sl.tile(LEAD["mixer"], TILES)
                if t:
                    dve.wait_ge(gates_ready, t.n + 1)
                    if t.first == 0:
                        dve.wait_ge(const_ready, 2)
                    else:
                        dve.wait_ge(hs_ready, t.n)
                        dve.wait_ge(carry_ready, t.n)
                    V.tensor_tensor_scan(hs[:, :], gate_a[:, :], gate_b[:, :], carry[:, :], ALU.mult, ALU.add)\
                     .then_inc(scan_done, 1)
                    dve.wait_ge(scan_done, t.n + 1)
                    if t.first:
                        dve.wait_ge(mixer_done, t.n)
                    V.tensor_scalar(hs_parts[0:S, :], hs[:, :], HS_SCALE, None, ALU.mult).then_inc(hs_hi, 1)
                    V.tensor_tensor(carry[:, :], hs[:, P - 1:P], keep[:, bass.ds(t.n + 1, 1)], ALU.mult)\
                     .then_inc(carry_ready, 1)
                    dve.wait_ge(hs_hi, t.n + 1)
                    V.scalar_tensor_tensor(hs_parts[S:P, :], hs[:, :], HS_SCALE, hs_parts[0:S, :],
                                           ALU.mult, ALU.subtract).then_inc(hs_ready, 1)
                    dve.wait_ge(mixer_done, t.n + 1)
                    dve.wait_ge(res1_ready, t.n + 1)
                    if t.first >= 2:
                        dve.wait_ge(ln_done[2], t.n - 1)
                        dve.wait_ge(bias_added, t.n - 1)
                    V.scalar_tensor_tensor(x_mid[:, t.odd, :], ps_c[:, :], wout_s[:, 4:5], x_in[:, t.odd, :],
                                           ALU.mult, ALU.add).then_inc(x1_ready, 1)
                    dve.wait_ge(x1_ready, t.n + 1)
                    moments(1, t, x_mid[:, t.odd, :])
                t = sl.tile(LEAD["attend"], TILES)
                if t:
                    if t.first == 0:
                        dve.wait_ge(f_allmax, 1)
                        power_scale(f_s, 1, RSQRT_R / XN_SCALE, f_step)
                        for n, k in enumerate(reversed(range(KD))):
                            dve.wait_ge(f_hi, n + 1)
                            V.scalar_tensor_tensor(f_part(k)[:, D:2 * D], f_store[:, k, :], f_s[:, 3:4],
                                                   f_part(k)[:, 0:D], ALU.mult, ALU.subtract).then_inc(f_lo, 1)
                    dve.wait_ge(xn_hi[2], t.n + 1)
                    low(xn3T[:, t.odd, 1, :], ps_t[:, :], xn3T[:, t.odd, 0, :]).then_inc(xnT_ready[2], 1)
                t = sl.tile(LEAD["probs"], TILES)
                if t:
                    dve.wait_ge(pt_hi_ready, t.n + 1)
                    cols = (slice(None), parity(t), slice(None), bass.ds(in_batch(t), P))
                    low(pt_lo[cols], blocks8(ps_c[:, :]), pt_hi[cols]).then_inc(pt_ready, 1)
                t = sl.tile(LEAD["ffn"], TILES)
                if t:
                    dve.wait_ge(ffn_done, t.n + 1)
                    dve.wait_ge(bias_added, t.n + 1)
                    V.scalar_tensor_tensor(x_out[:, t.odd, :], ps_ffn[:, :], f_s[:, 4:5], x_out[:, t.odd, :],
                                           ALU.mult, ALU.add).then_inc(out_ready, 1)
                t = sl.tile(LEAD["mixer"], TILES)
                if t:
                    dve.wait_ge(xn_hi[1], t.n + 1)
                    low(xn2T[:, 1, :], ps_t[:, :], xn2T[:, 0, :]).then_inc(xnT_ready[1], 1)
                t = sl.tile(LEAD["energy"], TILES)
                if t:
                    dve.wait_ge(energy_done, t.n + 1)
                    if t.first:
                        dve.wait_ge(exp_done, t.n)
                    V.tensor_reduce(neg_max[:, :], ps_c[:, :], AX.X, ALU.max, negate=True).then_inc(max_ready, 1)
                t = sl.tile(LEAD["ln1"], TILES)
                if t:
                    dve.wait_ge(x_loaded[t.odd], 16 * t.half + 16)
                    moments(0, t, x_in[:, t.odd, :])

            walk(dve, LEAD, TILES, body)

        @block.tensor
        def _(pe):
            mm = nc.tensor.matmul

            def turn(ps, src, n):
                for k in range(n):
                    last = nc.tensor.transpose(ps[:, k * P:(k + 1) * P], src[:, k * P:(k + 1) * P], ident[:, :])
                return last

            pe.wait_ge(ident_ready, 1)
            pe.wait_ge(wqk_loaded, 32)
            turn(ps_t, x_out[:, 0, :], 2 * KC).then_inc(w_psum, 1)
            pe.wait_ge(w_scaled, 1)
            turn(ps_c, wab_nat, KD).then_inc(w_psum, 1)
            pe.wait_ge(w_scaled, 2)
            turn(ps_attend, wout_nat, KD).then_inc(w_psum, 1)

            def products(ps, stat, mov, k0, k1, n_k):
                for k in range(k0, k1):
                    for n, (a, b) in enumerate(((0, 0), (0, 1), (1, 0))):
                        last = mm(ps, stat(k, a), mov(k, b), start=(k == 0 and n == 0),
                                  stop=(k == n_k - 1 and n == 2))
                return last

            def body(sl):
                tm, ta, tf = (sl.tile(LEAD[k], TILES) for k in ("mixer", "attend", "ffn"))
                tc, te, tp = (sl.tile(LEAD[k], TILES) for k in ("ctx", "energy", "probs"))

                def attend(h):
                    cols = slice(h * HALF, (h + 1) * HALF)
                    return products(ps_attend[:, cols], lambda k, a: xn2T[:, a, k * P:(k + 1) * P],
                                    lambda k, b: (pt_hi, pt_lo)[b][:, parity(ta), k, cols], 0, KD, KD)

                def ffn(h, k0, k1):
                    return products(ps_ffn[:, h * HALF:(h + 1) * HALF],
                                    lambda k, a: xn3T[:, tf.odd, a, k * P:(k + 1) * P],
                                    lambda k, b: f_part(k)[:, b * D + h * HALF:b * D + (h + 1) * HALF], k0, k1, KD)

                if ta:
                    pe.wait_ge(xnT_ready[1], ta.n + 1)
                    pe.wait_ge(pt_ready, batch_tiles(ta))
                    if ta.first:
                        pe.wait_ge(x2_ready, ta.n)
                    attend(0)
                if tm:
                    pe.wait_ge(ln_done[0], tm.n + 1)
                    if tm.first:
                        pe.wait_ge(xnT_ready[1], tm.n)
                    else:
                        pe.wait_ge(qk_ready, 2 * tc.n)
                    turn(ps_t, xn1, KD).then_inc(xn_turned[0], 1)
                if ta:
                    attend(1).then_inc(attend_done, 1)
                if tm:
                    pe.wait_ge(xnT_ready[0], tm.n + 1)
                    products(ps_t[:, 0:P], lambda k, a: wabT[:, a, k * P:(k + 1) * P],
                             lambda k, b: xn1T[:, b, k * P:(k + 1) * P], 0, KD, KD).then_inc(ab_done, 1)
                if tc:
                    pe.wait_ge(ctx_loaded[tc.odd], 16 * tc.half + 16)
                    if tc.first == 0:
                        pe.wait_ge(w_psum_read, 4)
                    turn(ps_t[:, HALF:2 * HALF], ctx_nat[:, tc.odd, :], KC).then_inc(ctx_turned, 1)
                if tf:
                    pe.wait_ge(xnT_ready[2], tf.n + 1)
                    if tf.first:
                        pe.wait_ge(out_ready, tf.n)
                    else:
                        pe.wait_ge(f_lo, KD)
                    ffn(0, 0, KD)
                if tm:
                    pe.wait_ge(hs_ready, tm.n + 1)
                    if te:
                        pe.wait_ge(exp_done, te.n)
                    elif tp:
                        pe.wait_ge(exp_done, TILES)
                    for h in range(2):
                        for part in range(2):
                            last = mm(ps_c[:, h * HALF:(h + 1) * HALF], hs_parts[:, :],
                                      woutT[:, part, h * HALF:(h + 1) * HALF], start=(part == 0), stop=(part == 1))
                    last.then_inc(mixer_done, 1)
                if tc:
                    pe.wait_ge(ctxT_ready, tc.n + 1)
                    if tc.first:
                        pe.wait_ge(qk_ready, 2 * tc.n)
                    for at, w in ((0, wqT), (P, wkT)):
                        for k in range(KC):
                            last = mm(ps_t[:, at:at + P], w[:, k * P:(k + 1) * P], ctxT[:, k * P:(k + 1) * P],
                                      start=(k == 0), stop=(k == KC - 1))
                    last.then_inc(qk_done, 1)
                if tf:
                    ffn(1, 0, KD // 2)
                if ta:
                    pe.wait_ge(ln_done[2], ta.n + 1)
                    if tc:
                        pe.wait_ge(qk_ready, 2 * tc.n + 2)
                    turn(ps_t, xn3, KD).then_inc(xn_turned[2], 1)
                if tp:
                    pe.wait_ge(probs_ready, tp.n + 1)
                    if tm:
                        pe.wait_ge(x1_ready, tm.n + 1)
                    turn(ps_c, probs, KD).then_inc(probs_turned, 1)
                if tf:
                    ffn(1, KD // 2, KD).then_inc(ffn_done, 1)
                if tm:
                    pe.wait_ge(ln_done[1], tm.n + 1)
                    if ta:
                        pe.wait_ge(xnT_ready[2], ta.n + 1)
                    elif tc:
                        pe.wait_ge(qk_ready, 2 * tc.n + 2)
                    turn(ps_t, xn2, KD).then_inc(xn_turned[1], 1)
                if te:
                    pe.wait_ge(q_tile_ready, te.n + 1)
                    pe.wait_ge(qk_ready, 2 * batch_tiles(te))
                    if tp:
                        pe.wait_ge(pt_ready, tp.n + 1)
                    for h in range(2):
                        last = mm(ps_c[:, h * HALF:(h + 1) * HALF], q_tile[:, :],
                                  kT[:, parity(te), h * HALF:(h + 1) * HALF], start=True, stop=True)
                    last.then_inc(energy_done, 1)

            walk(pe, LEAD, TILES, body)


_INS = ['x', 'ctx_1024', 'L0_attn_Wa', 'L0_attn_ba', 'L0_attn_Wb', 'L0_attn_bb', 'L0_attn_Wout', 'L0_attn_bout',
        'L0_xattn_Wq', 'L0_xattn_bq', 'L0_xattn_Wk', 'L0_xattn_bk', 'L0_ffn_factors', 'L0_ffn_bias']


def kernel(**inputs):
    import numpy as np
    import concourse.bacc as bacc
    from concourse.bass_utils import run_bass_kernel_spmd

    nc = bacc.Bacc("TRN2", target_bir_lowering=False, num_devices=1)
    arrays, args = {}, []
    for name in _INS:
        a = np.ascontiguousarray(inputs[name])
        arrays[f"in_{name}"] = a
        args.append(nc.dram_tensor(f"in_{name}", a.shape, mybir.dt.from_np(a.dtype), kind="ExternalInput").ap())
    shape = inputs['x'].shape
    args.append(nc.dram_tensor("out_0", shape, F32, kind="ExternalOutput").ap())
    decoder_kernel(nc, *args)
    r = run_bass_kernel_spmd(nc, [arrays], core_ids=[0])
    return r.results[0]["out_0"]
```

```python
from contextlib import ExitStack

import concourse.bass as bass
from concourse import mybir

ALU = mybir.AluOpType
ACT = mybir.ActivationFunctionType
AX = mybir.AxisListType
F32 = mybir.dt.float32
F16 = mybir.dt.float16
I32 = mybir.dt.int32

P = 128
HALF = 512
EPS = 1e-5
XN_SCALE = 2.0 ** 10
PROB_SCALE = 2.0 ** 15
HS_SCALE = 2.0 ** 4
W_TOP = 2.0 ** 14

LEAD = dict(turn_ctx=19, project=18, energy=10, scale_probs=9, probs=8, ln1=2, mixer=1, attend=0, ffn=-1)
LOADS = dict(ctx_load=21, x_load=3, store=-1, tokens=12)


class Tile:

    def __init__(self, half, odd, first):
        self.half, self.odd, self.first = half, odd, first

    @property
    def n(self):
        return 2 * self.half + self.odd


class Slice:

    def __init__(self, half, odd, first):
        self.half, self.odd, self.first = half, odd, first

    def tile(self, lead, tiles, start=0):
        first = self.first + lead
        if not start <= first < tiles:
            return None
        odd = (self.odd + lead) % 2
        return Tile(self.half + (self.odd + lead - odd) // 2, odd, first)


def walk(eng, leads, tiles, body, starts=None, counts=None, loops_from=None):
    starts, counts = starts or {}, counts or {}
    lo = min(starts.get(k, 0) - v for k, v in leads.items())
    hi = max(counts.get(k, tiles) - v for k, v in leads.items())

    def active(s):
        def state(k, v):
            t, t0 = s + v, starts.get(k, 0)
            return 0 if t < t0 or t >= counts.get(k, tiles) else (1 + t - t0 if t - t0 < 2 else 3)
        return tuple(state(k, v) for k, v in sorted(leads.items()))

    s = lo
    while s < hi:
        e = s
        while e < hi and active(e) == active(s):
            e += 1
        pairs = (e - s) // 2
        if pairs >= 2 and (loops_from is None or s >= loops_from):
            c, odd = s // 2, s % 2
            with eng.Fori(0, pairs) as i:
                body(Slice(i + c, odd, s))
                body(Slice(i + c + odd, 1 - odd, s + 1))
            s += 2 * pairs
        else:
            body(Slice(s // 2, s % 2, s))
            s += 1


def decoder_kernel(nc, x, ctx_in, wa, ba, wb, bb, wout, bout, wq, bq, wk, bk, factors, fbias, out):
    B, T, D = x.shape
    C = ctx_in.shape[2]
    S = wa.shape[0]
    R = factors.shape[0]
    TILES = B * T // P
    PER = T // P
    KD, KC = D // P, C // P
    assert 2 * S == P and wq.shape[0] == P and T == D == 2 * HALF and ctx_in.shape[1] == T and PER == 8
    RSQRT_R = float(R) ** -0.5

    x_rows = x.rearrange("b (j p) d -> (b j) p d", p=P)
    ctx_rows = ctx_in.rearrange("b (j p) c -> (b j) p c", p=P)
    out_rows = out.rearrange("b (j p) d -> (b j) p d", p=P)
    f_rows = factors.rearrange("r (a k p) e -> r a p k e", k=2, p=P)
    F_PARTS = KD // 2

    with ExitStack() as stack:
        def sb(name, shape, dt=F32):
            return stack.enter_context(nc.sbuf_tensor(name, shape, dt))

        def sem(name):
            return stack.enter_context(nc.semaphore(name))

        def psum(name):
            return stack.enter_context(nc.psum_tensor(name, [P, 2 * HALF], F32))

        ps_attend, ps_ffn, ps_c, ps_t = psum("ps_attend"), psum("ps_ffn"), psum("ps_c"), psum("ps_t")

        pt_hi = sb("pt_hi", [P, 2, KD, T], F16)
        pt_lo = sb("pt_lo", [P, 2, KD, T], F16)
        f_store = sb("f_store", [P, KD + 2, D])
        x_in = sb("x_in", [P, 2, D])
        x_mid = sb("x_mid", [P, 2, D])
        x_out = sb("x_out", [P, 2, D])
        xn12, xn3 = sb("xn12", [P, D]), sb("xn3", [P, D])
        xn1T = sb("xn1T", [P, 2, D], F16)
        xn2T = sb("xn2T", [P, 2, D], F16)
        xn3T = sb("xn3T", [P, 2, 2, D], F16)
        ctx_nat = sb("ctx_nat", [P, 2, C])
        ctxT = sb("ctxT", [P, 2, C])
        qT = sb("qT", [P, 2, T])
        kT = sb("kT", [P, 2, T])
        q_tile = sb("q_tile", [P, P])
        probs = sb("probs", [P, 2, T])
        wabT = sb("wabT", [P, 2, D], F16)
        woutT = sb("woutT", [P, 2, D], F16)
        wqT = sb("wqT", [P, C])
        wkT = sb("wkT", [P, C])
        wab_nat, wout_nat = x_mid[:, 0, :], x_mid[:, 1, :]
        wq_nat, wk_nat = x_out[:, 0, 0:C], x_out[:, 0, C:2 * C]
        bout_all = sb("bout_all", [P, D])
        fbias_all = sb("fbias_all", [P, D])
        ident = sb("ident", [P, P])
        bq_col, bk_col = sb("bq_col", [P, 1]), sb("bk_col", [P, 1])
        bab_col = sb("bab_col", [P, 1])
        gate_a = sb("gate_a", [S, P])
        gate_b = sb("gate_b", [S, P])
        hs = sb("hs", [S, P])
        hs_parts = sb("hs_parts", [P, P], F16)
        carry = sb("carry", [S, 1])
        keep = sb("keep", [S, TILES + 1])
        stats = sb("stats", [P, 3, 12])
        meanvar = sb("meanvar", [P, 3, 2])
        norm = sb("norm", [P, 3, 4])
        affine = sb("affine", [P, 2])
        f_most = sb("f_most", [P, F_PARTS])
        minus_half = sb("minus_half", [P, 1])
        neg_max = sb("neg_max", [P, 1])
        row_sum = sb("row_sum", [P, 1])
        row_inv = sb("row_inv", [P, 1])
        wab_s, wout_s, f_s = sb("wab_s", [P, 6]), sb("wout_s", [P, 6]), sb("f_s", [P, 6])

        wqk_loaded, wab_loaded, wout_loaded = sem("wqk_loaded"), sem("wab_loaded"), sem("wout_loaded")
        cols_loaded, rows_loaded = sem("cols_loaded"), sem("rows_loaded")
        f_loaded = [sem(f"f_loaded{a}") for a in range(F_PARTS)]
        x_loaded = [sem("x_loaded0"), sem("x_loaded1")]
        ctx_loaded = [sem("ctx_loaded0"), sem("ctx_loaded1")]
        stored = [sem("stored0"), sem("stored1")]
        ident_ready, const_ready, gp_const_ready = sem("ident_ready"), sem("const_ready"), sem("gp_const_ready")
        w_psum, w_psum_read = sem("w_psum"), sem("w_psum_read")
        wab_step, wout_step, f_step = sem("wab_step"), sem("wout_step"), sem("f_step")
        w_rowmax, w_allmax, w_scaled, w_hi = (
            sem("w_rowmax"), sem("w_allmax"), sem("w_scaled"), sem("w_hi"))
        f_max, f_allmax, f_hi, f_lo = sem("f_max"), sem("f_allmax"), sem("f_hi"), sem("f_lo")
        wait_carrier = sem("wait_carrier")
        ctx_turned, ctxT_ready, qk_done, qk_ready = (
            sem("ctx_turned"), sem("ctxT_ready"), sem("qk_done"), sem("qk_ready"))
        q_tile_ready, energy_done, max_ready, exp_done, inv_ready, probs_ready = (
            sem("q_tile_ready"), sem("energy_done"), sem("max_ready"), sem("exp_done"), sem("inv_ready"),
            sem("probs_ready"))
        probs_turned, pt_hi_ready, pt_ready = sem("probs_turned"), sem("pt_hi_ready"), sem("pt_ready")
        ln_parts = [sem(f"ln{k}_parts") for k in range(3)]
        ln_stats = [sem(f"ln{k}_stats") for k in range(3)]
        ln_var = [sem(f"ln{k}_var") for k in range(3)]
        ln_rstd = [sem(f"ln{k}_rstd") for k in range(3)]
        ln_scales = [sem(f"ln{k}_scales") for k in range(3)]
        ln_done = [sem(f"ln{k}_done") for k in range(3)]
        xn_turned = [sem(f"xn{k}_turned") for k in range(3)]
        xn_hi = [sem(f"xn{k}_hi") for k in range(3)]
        xnT_ready = [sem(f"xn{k}T_ready") for k in range(3)]
        affine_done, res1_ready = sem("affine_done"), sem("res1_ready")
        ab_done, gates_ready, scan_done, hs_hi, hs_ready, carry_ready = (
            sem("ab_done"), sem("gates_ready"), sem("scan_done"), sem("hs_hi"), sem("hs_ready"), sem("carry_ready"))
        mixer_done, x1_ready = sem("mixer_done"), sem("x1_ready")
        attend_done, x2_ready, bias_added, ffn_done, out_ready = (
            sem("attend_done"), sem("x2_ready"), sem("bias_added"), sem("ffn_done"), sem("out_ready"))

        blocks8 = lambda ap: ap.rearrange("p (k m) -> p k m", m=P)
        wout_4d = wout_nat.rearrange("p (k a s) -> p k a s", k=KD, a=2)
        f_part = lambda k: f_store[:, k + 2, :].bitcast(F16)
        xns = (xn12, xn12, xn3)

        def parity(t):
            return (t.half // (PER // 2)) % 2

        def in_batch(t):
            return (t.half % (PER // 2)) * (2 * P) + t.odd * P

        def batch_tiles(t):
            return (t.half // (PER // 2)) * PER + PER

        def ps_probs(sl):
            return ps_c if sl.tile(LEAD["ffn"], TILES) or sl.first > 0 else ps_ffn

        block = stack.enter_context(nc.Block())

        @block.sync
        def _(sp):
            sp.dma_start(wq_nat, wq).then_inc(wqk_loaded, 16)
            sp.dma_start(wk_nat, wk).then_inc(wqk_loaded, 16)
            for t in range(2):
                sp.dma_start(ctx_nat[:, t, :], ctx_rows[t]).then_inc(ctx_loaded[t], 16)
            with nc.allow_non_contiguous_dma(reason="bias columns, 128 words each"):
                sp.dma_start(bq_col[:, :], bq.rearrange("(p a) -> p a", a=1)).then_inc(cols_loaded, 16)
                sp.dma_start(bk_col[:, :], bk.rearrange("(p a) -> p a", a=1)).then_inc(cols_loaded, 16)
                sp.dma_start(bab_col[0:S, :], ba.rearrange("(p a) -> p a", a=1)).then_inc(cols_loaded, 16)
                sp.dma_start(bab_col[S:P, :], bb.rearrange("(p a) -> p a", a=1)).then_inc(cols_loaded, 16)
            sp.dma_start(wab_nat[0:S, :], wa).then_inc(wab_loaded, 16)
            sp.dma_start(wab_nat[S:P, :], wb).then_inc(wab_loaded, 16)
            for copy in range(2):
                sp.dma_start(wout_4d[:, :, copy, :], wout.rearrange("(k p) s -> p k s", p=P)).then_inc(wout_loaded, 16)

            def loads(sl):
                t = sl.tile(LOADS["ctx_load"], TILES, 2)
                if t:
                    sp.wait_ge(ctx_turned, t.n - 1)
                    sp.dma_start(ctx_nat[:, t.odd, :], ctx_rows[t.n]).then_inc(ctx_loaded[t.odd], 16)
                if sl.tile(LOADS["tokens"], 1):
                    for n in range(2):
                        sp.dma_start(x_in[:, n, :], x_rows[n]).then_inc(x_loaded[n], 16)
                    sp.dma_start(bout_all[:, :], bout.partition_broadcast(P)).then_inc(rows_loaded, 16)
                    sp.dma_start(fbias_all[:, :], fbias.partition_broadcast(P)).then_inc(rows_loaded, 16)
                t = sl.tile(LOADS["x_load"], TILES, 2)
                if t:
                    sp.wait_ge(x1_ready, t.n - 1)
                    sp.dma_start(x_in[:, t.odd, :], x_rows[t.n]).then_inc(x_loaded[t.odd], 16)
                t = sl.tile(LOADS["store"], TILES)
                if t:
                    sp.wait_ge(out_ready, t.n + 1)
                    sp.dma_start(out_rows[t.n], x_out[:, t.odd, :]).then_inc(stored[t.odd], 16)

            walk(sp, LOADS, TILES, loads, starts=dict(ctx_load=2, x_load=2), counts=dict(tokens=1))
            for odd in range(2):
                sp.wait_ge(stored[odd], 16 * TILES // 2)

        @block.gpsimd
        def _(gp):
            gp.memset(ident[:, :], 0.0).then_inc(gp_const_ready, 1)
            gp.memset(minus_half[:, :], -0.5).then_inc(gp_const_ready, 1)
            gp.wait_ge(gp_const_ready, 2)
            gp.affine_select(out=ident[:, :], in_=ident[:, :], compare_op=ALU.not_equal, fill=1.0, base=0,
                             pattern=[[-1, P]], channel_multiplier=1).then_inc(ident_ready, 1)

            def carry_wait():
                gp.sem_inc(wait_carrier, 1)

            def scales(k, t):
                gp.wait_ge(ln_stats[k], t.n + 1)
                if t.first:
                    gp.wait_ge(ln_done[k], t.n)
                carry_wait()
                gp.tensor_scalar(norm[:, k, 0:1], meanvar[:, k, 1:2], EPS, XN_SCALE ** -2, ALU.add, ALU.mult)\
                  .then_inc(ln_var[k], 1)
                gp.wait_ge(ln_var[k], t.n + 1)
                gp.tensor_tensor(norm[:, k, 1:2], norm[:, k, 0:1], minus_half[:, :], ALU.pow).then_inc(ln_rstd[k], 1)
                gp.wait_ge(ln_rstd[k], t.n + 1)
                carry_wait()
                gp.tensor_scalar(norm[:, k, 2:3], meanvar[:, k, 0:1], norm[:, k, 1:2], -1.0, ALU.mult, ALU.mult)\
                  .then_inc(ln_scales[k], 1)

            chunks = [(r, a) for r in range(R) for a in range(F_PARTS)]

            def add_factors(n):
                for r, a in chunks[:n]:
                    part = f_store[:, 2 * a:2 * a + 2, :]
                    if r:
                        gp.wait_ge(f_loaded[a], 16 * r)
                        gp.dma_start(part, f_rows[r, a], accum_op=ALU.add).then_inc(f_loaded[a], 16)
                    else:
                        gp.dma_start(part, f_rows[r, a]).then_inc(f_loaded[a], 16)
                del chunks[:n]

            gp.wait_ge(wqk_loaded, 32)
            gp.wait_ge(ctx_loaded[1], 16)

            def body(sl):
                if sl.first < -1:
                    add_factors(1)
                if sl.first == -16:
                    gp.wait_ge(w_rowmax, 2)
                    gp.partition_all_reduce(wout_s[:, 1:2], wout_s[:, 0:1], P, bass.bass_isa.ReduceOp.max)\
                      .then_inc(w_allmax, 1)
                if sl.first == 1:
                    gp.wait_ge(f_max, F_PARTS + 1)
                    gp.partition_all_reduce(f_s[:, 1:2], f_s[:, 0:1], P, bass.bass_isa.ReduceOp.max)\
                      .then_inc(f_allmax, 1)
                t = sl.tile(LEAD["energy"], TILES)
                if t:
                    gp.wait_ge(qk_ready, 2 * t.n + 2)
                    if t.first:
                        gp.wait_ge(energy_done, t.n)
                    gp.tensor_copy(q_tile[:, :], qT[:, parity(t), bass.ds(in_batch(t), P)]).then_inc(q_tile_ready, 1)
                t = sl.tile(LEAD["mixer"], TILES)
                if t:
                    gp.wait_ge(ln_done[0], t.n + 1)
                    carry_wait()
                    gp.tensor_scalar(affine[:, 0:1], norm[:, 0, 1:2], 1.0 / XN_SCALE, 1.0, ALU.mult, ALU.add)
                    gp.tensor_scalar(affine[:, 1:2], norm[:, 0, 2:3], 1.0 / XN_SCALE, 0.0, ALU.mult, ALU.add)\
                      .then_inc(affine_done, 1)
                    gp.wait_ge(affine_done, 2 * t.n + 1)
                    carry_wait()
                    gp.tensor_scalar(x_in[:, t.odd, :], x_in[:, t.odd, :], affine[:, 0:1], affine[:, 1:2],
                                     ALU.mult, ALU.add).then_inc(affine_done, 1)
                    if t.first == 0:
                        gp.wait_ge(rows_loaded, 32)
                    gp.wait_ge(affine_done, 2 * t.n + 2)
                    gp.tensor_tensor(x_in[:, t.odd, :], x_in[:, t.odd, :], bout_all[:, :], ALU.add)\
                      .then_inc(res1_ready, 1)
                if sl.first in (-1, 0):
                    add_factors(4)
                t = sl.tile(LEAD["scale_probs"], TILES)
                if t:
                    gp.wait_ge(inv_ready, t.n + 1)
                    carry_wait()
                    gp.tensor_scalar(probs[:, t.odd, :], probs[:, t.odd, :], row_inv[:, :], PROB_SCALE, ALU.mult, ALU.mult)\
                      .then_inc(probs_ready, 1)
                if sl.first in (-1, 0):
                    add_factors(2)
                t = sl.tile(LEAD["attend"], TILES)
                if t:
                    scales(2, t)
                    gp.wait_ge(x2_ready, t.n + 1)
                    if t.first >= 2:
                        gp.wait_ge(stored[t.odd], 16 * t.half)
                    gp.tensor_tensor(x_out[:, t.odd, :], x_mid[:, t.odd, :], fbias_all[:, :], ALU.add)\
                      .then_inc(bias_added, 1)
                t = sl.tile(LEAD["mixer"], TILES)
                if t:
                    scales(1, t)
                t = sl.tile(LEAD["ln1"], TILES)
                if t:
                    scales(0, t)
                if sl.first == -1:
                    add_factors(2)

            walk(gp, LEAD, TILES, body, loops_from=0)

        @block.scalar
        def _(act):
            def high(out_ap, psum_ap, scale=1.0):
                return nc.scalar.activation(out_ap, psum_ap, ACT.Copy, scale=scale)

            act.wait_ge(w_psum, 1)
            nc.scalar.copy(wqT[:, :], ps_t[:, 0:C]).then_inc(w_psum_read, 1)
            nc.scalar.copy(wkT[:, :], ps_t[:, C:2 * C]).then_inc(w_psum_read, 1)

            def normalise(k, t, src):
                act.wait_ge(ln_scales[k], t.n + 1)
                if k == 1:
                    act.wait_ge(xn_turned[0], t.n + 1)
                elif t.first:
                    act.wait_ge(xn_turned[1 if k == 0 else 2], t.n)
                nc.scalar.activation(xns[k][:, :], src, ACT.Identity, bias=norm[:, k, 2:3], scale=norm[:, k, 1:2])\
                  .then_inc(ln_done[k], 1)

            def split_factors(ks):
                for k in ks:
                    if k < KD - 2:
                        act.wait_ge(f_lo, KD - 2 - k)
                    nc.scalar.activation(f_part(k)[:, 0:D], f_store[:, k, :], ACT.Copy, scale=f_s[:, 3:4])\
                      .then_inc(f_hi, 1)

            def body(sl):
                ta = sl.tile(LEAD["attend"], TILES)
                if sl.first == -LEAD["energy"]:
                    act.wait_ge(w_psum, 2)
                    high(wabT[:, 0, :], ps_ffn[:, :]).then_inc(w_hi, 1)
                    act.wait_ge(w_psum, 3)
                    high(woutT[:, 0, :], ps_attend[:, :]).then_inc(w_hi, 1)
                if sl.first == 1:
                    act.wait_ge(f_step, 4)
                    split_factors(reversed(range(KD // 2, KD)))
                t = sl.tile(LEAD["mixer"], TILES)
                if t:
                    act.wait_ge(xn_turned[0], t.n + 1)
                    if t.first:
                        act.wait_ge(ab_done, t.n)
                    high(xn1T[:, 0, :], ps_t[:, :]).then_inc(xn_hi[0], 1)
                    if sl.first == 1:
                        split_factors(reversed(range(KD // 2)))
                    act.wait_ge(ab_done, t.n + 1)
                    if t.first == 0:
                        act.wait_ge(cols_loaded, 64)
                    if t.first:
                        act.wait_ge(scan_done, t.n)
                    nc.scalar.activation(gate_a[:, :], ps_t[0:S, 0:P], ACT.Tanh, bias=bab_col[0:S, :],
                                         scale=wab_s[0:S, 4:5])
                    nc.scalar.activation(gate_b[:, :], ps_t[S:P, 0:P], ACT.Tanh, bias=bab_col[S:P, :],
                                         scale=wab_s[S:P, 4:5]).then_inc(gates_ready, 1)
                t = sl.tile(LEAD["turn_ctx"], TILES)
                if t:
                    act.wait_ge(ctx_turned, t.n + 1)
                    if t.first >= 2:
                        act.wait_ge(qk_done, t.n - 1)
                    nc.scalar.copy(ctxT[:, t.odd, :], ps_t[:, HALF:HALF + C]).then_inc(ctxT_ready, 1)
                if ta:
                    normalise(2, ta, x_mid[:, ta.odd, :])
                t = sl.tile(LEAD["project"], TILES)
                if t:
                    act.wait_ge(qk_done, t.n + 1)
                    if t.first == 0:
                        act.wait_ge(cols_loaded, 64)
                    if t.first > PER:
                        act.wait_ge(energy_done, t.n - PER)
                    for dst, at, bias in ((qT, 0, bq_col), (kT, P, bk_col)):
                        nc.scalar.activation(dst[:, parity(t), bass.ds(in_batch(t), P)], ps_t[:, at:at + P],
                                             ACT.Identity, bias=bias[:, :]).then_inc(qk_ready, 1)
                t = sl.tile(LEAD["mixer"], TILES)
                if t:
                    normalise(1, t, x_mid[:, t.odd, :])
                if ta:
                    act.wait_ge(xn_turned[2], ta.n + 1)
                    if ta.first >= 2:
                        act.wait_ge(ffn_done, ta.n - 1)
                    high(xn3T[:, ta.odd, 0, :], ps_t[:, :]).then_inc(xn_hi[2], 1)
                t = sl.tile(LEAD["probs"], TILES)
                if t:
                    act.wait_ge(probs_turned, t.n + 1)
                    if t.first > PER:
                        act.wait_ge(attend_done, t.n - PER)
                    high(pt_hi[:, parity(t), :, bass.ds(in_batch(t), P)], blocks8(ps_probs(sl)[:, :]))\
                        .then_inc(pt_hi_ready, 1)
                t = sl.tile(LEAD["mixer"], TILES)
                if t:
                    act.wait_ge(xn_turned[1], t.n + 1)
                    if t.first:
                        act.wait_ge(attend_done, t.n)
                    high(xn2T[:, 0, :], ps_t[:, :]).then_inc(xn_hi[1], 1)
                t = sl.tile(LEAD["energy"], TILES)
                if t:
                    act.wait_ge(max_ready, t.n + 1)
                    if t.first >= 2:
                        act.wait_ge(probs_turned, t.n - 1)
                    if t.first:
                        act.wait_ge(inv_ready, t.n)
                    nc.scalar.activation(probs[:, t.odd, :], ps_c[:, :], ACT.Exp, bias=neg_max[:, :],
                                         accum_out=row_sum[:, :]).then_inc(exp_done, 1)
                t = sl.tile(LEAD["ln1"], TILES)
                if t:
                    normalise(0, t, x_in[:, t.odd, :])

            walk(act, LEAD, TILES, body)

        @block.vector
        def _(dve):
            V = nc.vector
            V.memset(keep[:, :], 1.0).then_inc(const_ready, 1)
            dve.wait_ge(const_ready, 1)
            V.memset(keep[:, 0:TILES + 1:PER], 0.0)
            V.memset(carry[:, :], 0.0).then_inc(const_ready, 1)

            def power_scale(s, src, carried, step):
                V.tensor_scalar(s[:, 2:3], s[:, src:src + 1], 1e-30, None, ALU.max).then_inc(step, 1)
                dve.wait_ge(step, 1)
                V.tensor_scalar(s[:, 5:6].bitcast(I32), s[:, 2:3].bitcast(I32), 0x7F800000, None, ALU.bitwise_and)\
                 .then_inc(step, 1)
                dve.wait_ge(step, 2)
                V.tensor_scalar(s[:, 4:5], s[:, 5:6], carried / W_TOP, None, ALU.mult)
                V.tensor_scalar(s[:, 2:3], s[:, 5:6], 1.0 / W_TOP, None, ALU.mult).then_inc(step, 1)
                dve.wait_ge(step, 3)
                V.reciprocal(s[:, 3:4], s[:, 2:3]).then_inc(step, 1)
                dve.wait_ge(step, 4)

            dve.wait_ge(wab_loaded, 32)
            V.tensor_reduce(wab_s[:, 0:1], wab_nat, AX.X, ALU.max, apply_absolute_value=True)\
             .then_inc(w_rowmax, 1)
            dve.wait_ge(wout_loaded, 32)
            V.tensor_reduce(wout_s[:, 0:1], wout_nat, AX.X, ALU.max, apply_absolute_value=True)\
             .then_inc(w_rowmax, 1)
            dve.wait_ge(w_rowmax, 1)
            power_scale(wab_s, 0, 1.0 / XN_SCALE, wab_step)
            V.tensor_scalar(wab_nat, wab_nat, wab_s[:, 3:4], None, ALU.mult).then_inc(w_scaled, 1)
            dve.wait_ge(w_allmax, 1)
            power_scale(wout_s, 1, 1.0 / HS_SCALE, wout_step)
            V.tensor_scalar(wout_nat, wout_nat, wout_s[:, 3:4], None, ALU.mult).then_inc(w_scaled, 1)
            def low(out_ap, psum_ap, high_ap):
                return V.tensor_tensor(out_ap, psum_ap, high_ap, ALU.subtract)

            def moments(k, t, src):
                if t.first:
                    dve.wait_ge(ln_scales[k], t.n)
                for h in range(2):
                    V.bn_stats(stats[:, k, 6 * h:6 * h + 6], src[:, h * HALF:(h + 1) * HALF]).then_inc(ln_parts[k], 1)
                dve.wait_ge(ln_parts[k], 2 * t.n + 2)
                dve.sem_inc(wait_carrier, 1)
                V.bn_aggr(meanvar[:, k, :], stats[:, k, :]).then_inc(ln_stats[k], 1)

            def factors_max(parts):
                for a in parts:
                    dve.wait_ge(f_loaded[a], 16 * R)
                    V.tensor_reduce(f_most[:, a:a + 1], f_store[:, 2 * a:2 * a + 2, :], AX.XY, ALU.max,
                                    apply_absolute_value=True).then_inc(f_max, 1)

            def split_factors(ks):
                for k in ks:
                    dve.wait_ge(f_hi, KD - k)
                    V.scalar_tensor_tensor(f_part(k)[:, D:2 * D], f_store[:, k, :], f_s[:, 3:4],
                                           f_part(k)[:, 0:D], ALU.mult, ALU.subtract).then_inc(f_lo, 1)

            def body(sl):
                ta = sl.tile(LEAD["attend"], TILES)
                tm = sl.tile(LEAD["mixer"], TILES)
                if sl.first == -LEAD["energy"]:
                    dve.wait_ge(w_hi, 1)
                    low(wabT[:, 1, :], ps_ffn[:, :], wabT[:, 0, :]).then_inc(w_psum_read, 1)
                    dve.wait_ge(w_hi, 2)
                    low(woutT[:, 1, :], ps_attend[:, :], woutT[:, 0, :]).then_inc(w_psum_read, 1)
                t = sl.tile(LEAD["scale_probs"], TILES)
                if t:
                    dve.wait_ge(exp_done, t.n + 1)
                    if t.first:
                        dve.wait_ge(probs_ready, t.n)
                    V.reciprocal(row_inv[:, :], row_sum[:, :]).then_inc(inv_ready, 1)
                if sl.first == 1:
                    factors_max((F_PARTS - 1,))
                    dve.wait_ge(f_max, F_PARTS)
                    V.tensor_reduce(f_s[:, 0:1], f_most[:, :], AX.X, ALU.max).then_inc(f_max, 1)
                    dve.wait_ge(f_allmax, 1)
                    power_scale(f_s, 1, RSQRT_R / XN_SCALE, f_step)
                    split_factors(reversed(range(KD // 2, KD)))
                if tm:
                    dve.wait_ge(xn_hi[0], tm.n + 1)
                    low(xn1T[:, 1, :], ps_t[:, :], xn1T[:, 0, :]).then_inc(xnT_ready[0], 1)
                if sl.first == 1:
                    split_factors(reversed(range(KD // 2)))
                if ta:
                    dve.wait_ge(attend_done, ta.n + 1)
                    mid = x_mid[:, ta.odd, :]
                    V.scalar_tensor_tensor(mid, ps_attend[:, :], 1.0 / (XN_SCALE * PROB_SCALE), mid, ALU.mult, ALU.add)\
                     .then_inc(x2_ready, 1)
                if tm:
                    dve.wait_ge(gates_ready, tm.n + 1)
                    if tm.first == 0:
                        dve.wait_ge(const_ready, 2)
                    else:
                        dve.wait_ge(hs_ready, tm.n)
                        dve.wait_ge(carry_ready, tm.n)
                    V.tensor_tensor_scan(hs[:, :], gate_a[:, :], gate_b[:, :], carry[:, :], ALU.mult, ALU.add)\
                     .then_inc(scan_done, 1)
                    dve.wait_ge(scan_done, tm.n + 1)
                    if tm.first:
                        dve.wait_ge(mixer_done, tm.n)
                    V.tensor_scalar(hs_parts[0:S, :], hs[:, :], HS_SCALE, None, ALU.mult).then_inc(hs_hi, 1)
                    V.tensor_tensor(carry[:, :], hs[:, P - 1:P], keep[:, bass.ds(tm.n + 1, 1)], ALU.mult)\
                     .then_inc(carry_ready, 1)
                    dve.wait_ge(hs_hi, tm.n + 1)
                    V.scalar_tensor_tensor(hs_parts[S:P, :], hs[:, :], HS_SCALE, hs_parts[0:S, :],
                                           ALU.mult, ALU.subtract).then_inc(hs_ready, 1)
                if ta:
                    dve.wait_ge(x2_ready, ta.n + 1)
                    moments(2, ta, mid)
                if tm:
                    dve.wait_ge(mixer_done, tm.n + 1)
                    dve.wait_ge(res1_ready, tm.n + 1)
                    if tm.first >= 2:
                        dve.wait_ge(ln_done[2], tm.n - 1)
                        dve.wait_ge(bias_added, tm.n - 1)
                    V.scalar_tensor_tensor(x_mid[:, tm.odd, :], ps_c[:, :], wout_s[:, 4:5], x_in[:, tm.odd, :],
                                           ALU.mult, ALU.add).then_inc(x1_ready, 1)
                    dve.wait_ge(x1_ready, tm.n + 1)
                    moments(1, tm, x_mid[:, tm.odd, :])
                if ta:
                    dve.wait_ge(xn_hi[2], ta.n + 1)
                    low(xn3T[:, ta.odd, 1, :], ps_t[:, :], xn3T[:, ta.odd, 0, :]).then_inc(xnT_ready[2], 1)
                t = sl.tile(LEAD["probs"], TILES)
                if t:
                    dve.wait_ge(pt_hi_ready, t.n + 1)
                    cols = (slice(None), parity(t), slice(None), bass.ds(in_batch(t), P))
                    low(pt_lo[cols], blocks8(ps_probs(sl)[:, :]), pt_hi[cols]).then_inc(pt_ready, 1)
                if tm:
                    dve.wait_ge(xn_hi[1], tm.n + 1)
                    low(xn2T[:, 1, :], ps_t[:, :], xn2T[:, 0, :]).then_inc(xnT_ready[1], 1)
                t = sl.tile(LEAD["ffn"], TILES)
                if t:
                    dve.wait_ge(ffn_done, t.n + 1)
                    dve.wait_ge(bias_added, t.n + 1)
                    V.scalar_tensor_tensor(x_out[:, t.odd, :], ps_ffn[:, :], f_s[:, 4:5], x_out[:, t.odd, :],
                                           ALU.mult, ALU.add).then_inc(out_ready, 1)
                t = sl.tile(LEAD["energy"], TILES)
                if t:
                    dve.wait_ge(energy_done, t.n + 1)
                    if t.first:
                        dve.wait_ge(exp_done, t.n)
                    V.tensor_reduce(neg_max[:, :], ps_c[:, :], AX.X, ALU.max, negate=True).then_inc(max_ready, 1)
                t = sl.tile(LEAD["ln1"], TILES)
                if t:
                    dve.wait_ge(x_loaded[t.odd], 16 * t.half + 16)
                    moments(0, t, x_in[:, t.odd, :])
                if sl.first == 0:
                    factors_max(range(F_PARTS - 1))

            walk(dve, LEAD, TILES, body)

        @block.tensor
        def _(pe):
            mm = nc.tensor.matmul

            def turn(ps, src, n):
                for k in range(n):
                    last = nc.tensor.transpose(ps[:, k * P:(k + 1) * P], src[:, k * P:(k + 1) * P], ident[:, :])
                return last

            pe.wait_ge(ident_ready, 1)
            pe.wait_ge(wqk_loaded, 32)
            turn(ps_t, x_out[:, 0, :], 2 * KC).then_inc(w_psum, 1)
            def products(ps, stat, mov, k0, k1, n_k):
                for k in range(k0, k1):
                    for n, (a, b) in enumerate(((0, 0), (0, 1), (1, 0))):
                        last = mm(ps, stat(k, a), mov(k, b), start=(k == 0 and n == 0),
                                  stop=(k == n_k - 1 and n == 2))
                return last

            def body(sl):
                tm, ta, tf = (sl.tile(LEAD[k], TILES) for k in ("mixer", "attend", "ffn"))
                tt, tc, te, tp = (sl.tile(LEAD[k], TILES) for k in ("turn_ctx", "project", "energy", "probs"))
                if te and te.first == 0:
                    pe.wait_ge(w_scaled, 1)
                    turn(ps_ffn, wab_nat, KD).then_inc(w_psum, 1)
                    pe.wait_ge(w_scaled, 2)
                    turn(ps_attend, wout_nat, KD).then_inc(w_psum, 1)

                def attend(h):
                    cols = slice(h * HALF, (h + 1) * HALF)
                    return products(ps_attend[:, cols], lambda k, a: xn2T[:, a, k * P:(k + 1) * P],
                                    lambda k, b: (pt_hi, pt_lo)[b][:, parity(ta), k, cols], 0, KD, KD)

                def ffn(h, k0, k1):
                    return products(ps_ffn[:, h * HALF:(h + 1) * HALF],
                                    lambda k, a: xn3T[:, tf.odd, a, k * P:(k + 1) * P],
                                    lambda k, b: f_part(k)[:, b * D + h * HALF:b * D + (h + 1) * HALF], k0, k1, KD)

                if ta:
                    pe.wait_ge(xnT_ready[1], ta.n + 1)
                    pe.wait_ge(pt_ready, batch_tiles(ta))
                    if ta.first:
                        pe.wait_ge(x2_ready, ta.n)
                    attend(0)
                if tm:
                    pe.wait_ge(ln_done[0], tm.n + 1)
                    if tm.first:
                        pe.wait_ge(xnT_ready[1], tm.n)
                    else:
                        pe.wait_ge(qk_ready, 2 * tc.n)
                        pe.wait_ge(ctxT_ready, tt.n)
                    turn(ps_t, xn12, KD).then_inc(xn_turned[0], 1)
                if ta:
                    attend(1).then_inc(attend_done, 1)
                if tm:
                    pe.wait_ge(xnT_ready[0], tm.n + 1)
                    products(ps_t[:, 0:P], lambda k, a: wabT[:, a, k * P:(k + 1) * P],
                             lambda k, b: xn1T[:, b, k * P:(k + 1) * P], 0, KD, KD).then_inc(ab_done, 1)
                if tt:
                    pe.wait_ge(ctx_loaded[tt.odd], 16 * tt.half + 16)
                    if tt.first:
                        pe.wait_ge(ctxT_ready, tt.n)
                    else:
                        pe.wait_ge(w_psum_read, 2)
                    turn(ps_t[:, HALF:2 * HALF], ctx_nat[:, tt.odd, :], KC).then_inc(ctx_turned, 1)
                if tf:
                    pe.wait_ge(xnT_ready[2], tf.n + 1)
                    if tf.first:
                        pe.wait_ge(out_ready, tf.n)
                    else:
                        pe.wait_ge(pt_ready, tp.n)
                        pe.wait_ge(f_lo, KD)
                    ffn(0, 0, KD // 2)
                if tm:
                    pe.wait_ge(hs_ready, tm.n + 1)
                    if te and te.first:
                        pe.wait_ge(exp_done, te.n)
                    elif not te and sl.tile(LEAD["scale_probs"], TILES):
                        pe.wait_ge(exp_done, TILES)
                    for h in range(2):
                        for part in range(2):
                            last = mm(ps_c[:, h * HALF:(h + 1) * HALF], hs_parts[:, :],
                                      woutT[:, part, h * HALF:(h + 1) * HALF], start=(part == 0), stop=(part == 1))
                    last.then_inc(mixer_done, 1)
                if tc:
                    pe.wait_ge(ctxT_ready, tc.n + 1)
                    if tc.first:
                        pe.wait_ge(qk_ready, 2 * tc.n)
                    else:
                        pe.wait_ge(w_psum_read, 2)
                    for at, w in ((0, wqT), (P, wkT)):
                        for k in range(KC):
                            last = mm(ps_t[:, at:at + P], w[:, k * P:(k + 1) * P],
                                      ctxT[:, tc.odd, k * P:(k + 1) * P], start=(k == 0), stop=(k == KC - 1))
                    last.then_inc(qk_done, 1)
                if tf:
                    ffn(0, KD // 2, KD)
                if ta:
                    pe.wait_ge(ln_done[2], ta.n + 1)
                    if tc:
                        pe.wait_ge(qk_ready, 2 * tc.n + 2)
                    if tt:
                        pe.wait_ge(ctxT_ready, tt.n + 1)
                    turn(ps_t, xn3, KD).then_inc(xn_turned[2], 1)
                if tp:
                    pe.wait_ge(probs_ready, tp.n + 1)
                    if ps_probs(sl) is ps_c:
                        if tm:
                            pe.wait_ge(x1_ready, tm.n + 1)
                    elif tp.first:
                        pe.wait_ge(pt_ready, tp.n)
                    else:
                        pe.wait_ge(w_psum_read, 4)
                    turn(ps_probs(sl), probs[:, tp.odd, :], KD).then_inc(probs_turned, 1)
                if tf:
                    ffn(1, 0, KD // 2)
                if tm:
                    pe.wait_ge(ln_done[1], tm.n + 1)
                    if ta:
                        pe.wait_ge(xnT_ready[2], ta.n + 1)
                    else:
                        pe.wait_ge(qk_ready, 2 * tc.n + 2)
                        pe.wait_ge(ctxT_ready, tt.n + 1)
                    turn(ps_t, xn12, KD).then_inc(xn_turned[1], 1)
                if tf:
                    ffn(1, KD // 2, KD).then_inc(ffn_done, 1)
                if te:
                    pe.wait_ge(q_tile_ready, te.n + 1)
                    pe.wait_ge(qk_ready, 2 * batch_tiles(te))
                    if te.first:
                        pe.wait_ge(exp_done, te.n)
                    if tm:
                        pe.wait_ge(x1_ready, tm.n + 1)
                    if tp and ps_probs(sl) is ps_c:
                        pe.wait_ge(pt_ready, tp.n + 1)
                    for h in range(2):
                        last = mm(ps_c[:, h * HALF:(h + 1) * HALF], q_tile[:, :],
                                  kT[:, parity(te), h * HALF:(h + 1) * HALF], start=True, stop=True)
                    last.then_inc(energy_done, 1)

            walk(pe, LEAD, TILES, body)


_INS = ['x', 'ctx_1024', 'L0_attn_Wa', 'L0_attn_ba', 'L0_attn_Wb', 'L0_attn_bb', 'L0_attn_Wout', 'L0_attn_bout',
        'L0_xattn_Wq', 'L0_xattn_bq', 'L0_xattn_Wk', 'L0_xattn_bk', 'L0_ffn_factors', 'L0_ffn_bias']


def kernel(**inputs):
    import numpy as np
    import concourse.bacc as bacc
    from concourse.bass_utils import run_bass_kernel_spmd

    nc = bacc.Bacc("TRN2", target_bir_lowering=False, num_devices=1)
    arrays, args = {}, []
    for name in _INS:
        a = np.ascontiguousarray(inputs[name])
        arrays[f"in_{name}"] = a
        args.append(nc.dram_tensor(f"in_{name}", a.shape, mybir.dt.from_np(a.dtype), kind="ExternalInput").ap())
    shape = inputs['x'].shape
    args.append(nc.dram_tensor("out_0", shape, F32, kind="ExternalOutput").ap())
    decoder_kernel(nc, *args)
    r = run_bass_kernel_spmd(nc, [arrays], core_ids=[0])
    return r.results[0]["out_0"]
```

```python
from contextlib import ExitStack

import concourse.bass as bass
from concourse import mybir

ALU = mybir.AluOpType
ACT = mybir.ActivationFunctionType
AX = mybir.AxisListType
F32 = mybir.dt.float32
F16 = mybir.dt.float16
I32 = mybir.dt.int32

P = 128
HALF = 512
EPS = 1e-5
XN_SCALE = 2.0 ** 10
PROB_SCALE = 2.0 ** 15
HS_SCALE = 2.0 ** 4
W_TOP = 2.0 ** 14

LEAD = dict(turn_ctx=19, project=18, q_tile=11, energy=10, scale_probs=9, probs=8, ln1=2, mixer=1, attend=0, ffn=-1)
EARLY = dict(ln1=7, norm1=6, turn1=5, gates=4, output=2, norm2=1, turn2=1)
LOADS = dict(ctx_load=21, x_load=3, store=-1, x_first=11, rows=6)
FACTORS_MAX, FACTORS_SPLIT = 1, 2
CHUNKS_AT_START = {s: 1 for s in (*range(-LEAD["turn_ctx"], -12), -5, -3)} | {0: 3}
CHUNKS_AFTER_SCALING = {s: 2 if s in (-7, -2, -1) else 1 for s in range(-11, 0)} | {0: 2}
WOUT_MAX = -16


class Tile:

    def __init__(self, half, odd, first):
        self.half, self.odd, self.first = half, odd, first

    @property
    def n(self):
        return 2 * self.half + self.odd


class Slice:

    def __init__(self, half, odd, first):
        self.half, self.odd, self.first = half, odd, first

    def tile(self, lead, tiles, start=0):
        first = self.first + lead
        if not start <= first < tiles:
            return None
        odd = (self.odd + lead) % 2
        return Tile(self.half + (self.odd + lead - odd) // 2, odd, first)

    def step(self, name, tiles):
        if self.first == -EARLY[name]:
            return Tile(0, 0, 0)
        return self.tile(LEAD["ln1" if name in ("ln1", "norm1") else "mixer"], tiles, 1)


def walk(eng, leads, tiles, body, starts=None, counts=None):
    starts, counts = starts or {}, counts or {}
    lo = min(starts.get(k, 0) - v for k, v in leads.items())
    hi = max(counts.get(k, tiles) - v for k, v in leads.items())

    def active(s):
        def state(k, v):
            t, t0 = s + v, starts.get(k, 0)
            return 0 if t < t0 or t >= counts.get(k, tiles) else (1 + t - t0 if t - t0 < 2 else 3)
        alone = s if s < 0 else None
        return (alone,) + tuple(state(k, v) for k, v in sorted(leads.items()))

    s = lo
    while s < hi:
        e = s
        while e < hi and active(e) == active(s):
            e += 1
        pairs = (e - s) // 2
        if pairs >= 2:
            c, odd = s // 2, s % 2
            with eng.Fori(0, pairs) as i:
                body(Slice(i + c, odd, s))
                body(Slice(i + c + odd, 1 - odd, s + 1))
            s += 2 * pairs
        else:
            body(Slice(s // 2, s % 2, s))
            s += 1


def decoder_kernel(nc, x, ctx_in, wa, ba, wb, bb, wout, bout, wq, bq, wk, bk, factors, fbias, out):
    B, T, D = x.shape
    C = ctx_in.shape[2]
    S = wa.shape[0]
    R = factors.shape[0]
    TILES = B * T // P
    PER = T // P
    KD, KC = D // P, C // P
    assert 2 * S == P and wq.shape[0] == P and T == D == 2 * HALF and ctx_in.shape[1] == T and PER == 8
    CTX_FIRST, CTX_PIECE = 2 * PER, PER // 2
    RSQRT_R = float(R) ** -0.5

    x_rows = x.rearrange("b (j p) d -> (b j) p d", p=P)
    ctx_rows = ctx_in.rearrange("b (j p) c -> (b j) p c", p=P)
    out_rows = out.rearrange("b (j p) d -> (b j) p d", p=P)
    f_rows = factors.rearrange("r (a k p) e -> r a p k e", k=2, p=P)
    F_PARTS = KD // 2

    with ExitStack() as stack:
        def sb(name, shape, dt=F32):
            return stack.enter_context(nc.sbuf_tensor(name, shape, dt))

        def sem(name):
            return stack.enter_context(nc.semaphore(name))

        def psum(name):
            return stack.enter_context(nc.psum_tensor(name, [P, 2 * HALF], F32))

        ps_attend, ps_ffn, ps_c, ps_t = psum("ps_attend"), psum("ps_ffn"), psum("ps_c"), psum("ps_t")

        pt_hi = sb("pt_hi", [P, 2, KD, T], F16)
        pt_lo = sb("pt_lo", [P, 2, KD, T], F16)
        f_store = sb("f_store", [P, KD + 2, D])
        x_in = sb("x_in", [P, 2, D])
        x_mid = sb("x_mid", [P, 2, D])
        x_out = sb("x_out", [P, 2, D])
        xn12, xn3 = sb("xn12", [P, D]), sb("xn3", [P, D])
        xn1T = sb("xn1T", [P, 2, D], F16)
        xn2T = sb("xn2T", [P, 2, D], F16)
        xn3T = sb("xn3T", [P, 2, 2, D], F16)
        ctx_nat = sb("ctx_nat", [P, 2, C])
        ctxT = sb("ctxT", [P, 2, C])
        qT = sb("qT", [P, 2, T])
        kT = sb("kT", [P, 2, T])
        q_tile = sb("q_tile", [P, 2, P])
        probs = sb("probs", [P, 2, T])
        wabT = sb("wabT", [P, 2, D], F16)
        woutT = sb("woutT", [P, 2, D], F16)
        wqT = sb("wqT", [P, C])
        wkT = sb("wkT", [P, C])
        wab_nat, wout_nat = x_mid[:, 0, :], x_mid[:, 1, :]
        wq_nat, wk_nat = x_out[:, 0, 0:C], x_out[:, 0, C:2 * C]
        ctx_first = [ap[:, 1, :, :].rearrange("p k t -> p (k t)").bitcast(F32).rearrange("p (j c) -> p j c", c=C)
                     for ap in (pt_hi, pt_lo)]
        bout_all = sb("bout_all", [P, D])
        fbias_all = sb("fbias_all", [P, D])
        ident = sb("ident", [P, P])
        bq_col, bk_col = sb("bq_col", [P, 1]), sb("bk_col", [P, 1])
        bab_col = sb("bab_col", [P, 1])
        gate_a = sb("gate_a", [S, P])
        gate_b = sb("gate_b", [S, P])
        hs = gate_b
        hs_parts = sb("hs_parts", [P, P], F16)
        carry = sb("carry", [S, 1])
        keep = sb("keep", [S, TILES + 1])
        stats = sb("stats", [P, 3, 12])
        meanvar = sb("meanvar", [P, 3, 2])
        norm = sb("norm", [P, 3, 4])
        affine = sb("affine", [P, 2])
        f_most = sb("f_most", [P, F_PARTS])
        minus_half = sb("minus_half", [P, 1])
        neg_max = sb("neg_max", [P, 1])
        row_sum = sb("row_sum", [P, 1])
        row_inv = sb("row_inv", [P, 1])
        wab_s, wout_s, f_s = sb("wab_s", [P, 6]), sb("wout_s", [P, 6]), sb("f_s", [P, 6])

        wqk_loaded, wab_loaded, wout_loaded = sem("wqk_loaded"), sem("wab_loaded"), sem("wout_loaded")
        cols_loaded, rows_loaded = sem("cols_loaded"), sem("rows_loaded")
        f_loaded = [sem(f"f_loaded{a}") for a in range(F_PARTS)]
        x_loaded = [sem("x_loaded0"), sem("x_loaded1")]
        ctx_loaded = [sem("ctx_loaded0"), sem("ctx_loaded1")]
        ctx_first_loaded = [sem(f"ctx_first_loaded{a}") for a in range(CTX_FIRST // CTX_PIECE)]
        stored = [sem("stored0"), sem("stored1")]
        ident_ready, const_ready, gp_const_ready = sem("ident_ready"), sem("const_ready"), sem("gp_const_ready")
        w_psum, w_psum_read = sem("w_psum"), sem("w_psum_read")
        wab_step, wout_step, f_step = sem("wab_step"), sem("wout_step"), sem("f_step")
        w_rowmax, w_allmax, w_scaled, w_hi = (
            sem("w_rowmax"), sem("w_allmax"), sem("w_scaled"), sem("w_hi"))
        f_max, f_allmax, f_hi, f_lo = sem("f_max"), sem("f_allmax"), sem("f_hi"), sem("f_lo")
        wait_carrier = sem("wait_carrier")
        ctx_turned, ctxT_ready, qk_done, qk_ready = (
            sem("ctx_turned"), sem("ctxT_ready"), sem("qk_done"), sem("qk_ready"))
        q_tile_ready, energy_done, max_ready, exp_done, inv_ready, probs_ready = (
            sem("q_tile_ready"), sem("energy_done"), sem("max_ready"), sem("exp_done"), sem("inv_ready"),
            sem("probs_ready"))
        probs_turned, pt_hi_ready, pt_ready = sem("probs_turned"), sem("pt_hi_ready"), sem("pt_ready")
        ln_parts = [sem(f"ln{k}_parts") for k in range(3)]
        ln_stats = [sem(f"ln{k}_stats") for k in range(3)]
        ln_var = [sem(f"ln{k}_var") for k in range(3)]
        ln_rstd = [sem(f"ln{k}_rstd") for k in range(3)]
        ln_scales = [sem(f"ln{k}_scales") for k in range(3)]
        ln_done = [sem(f"ln{k}_done") for k in range(3)]
        xn_turned = [sem(f"xn{k}_turned") for k in range(3)]
        xn_hi = [sem(f"xn{k}_hi") for k in range(3)]
        xnT_ready = [sem(f"xn{k}T_ready") for k in range(3)]
        affine_done, res1_ready = sem("affine_done"), sem("res1_ready")
        ab_done, gates_ready, scan_done, hs_hi, hs_ready, carry_ready = (
            sem("ab_done"), sem("gates_ready"), sem("scan_done"), sem("hs_hi"), sem("hs_ready"), sem("carry_ready"))
        mixer_done, x1_ready = sem("mixer_done"), sem("x1_ready")
        attend_done, x2_ready, bias_added, ffn_done, out_ready = (
            sem("attend_done"), sem("x2_ready"), sem("bias_added"), sem("ffn_done"), sem("out_ready"))

        blocks8 = lambda ap: ap.rearrange("p (k m) -> p k m", m=P)
        wout_4d = wout_nat.rearrange("p (k a s) -> p k a s", k=KD, a=2)
        f_part = lambda k: f_store[:, k + 2, :].bitcast(F16)
        xns = (xn12, xn12, xn3)

        def parity(t):
            return (t.half // (PER // 2)) % 2

        def in_batch(t):
            return (t.half % (PER // 2)) * (2 * P) + t.odd * P

        def batch_tiles(t):
            return (t.half // (PER // 2)) * PER + PER

        def ps_probs(sl):
            return ps_c if sl.first >= FACTORS_SPLIT else ps_ffn

        def ps_project(t):
            return ps_c if t.first < PER and t.odd else ps_t

        def ps_energy(t):
            return ps_attend if t.first < LEAD["energy"] and not t.odd else ps_c

        def ps_gates(t):
            return ps_t if t.first else ps_c

        def ps_xn1(t):
            return ps_t if t.first else ps_attend

        block = stack.enter_context(nc.Block())

        @block.sync
        def _(sp):
            sp.dma_start(wq_nat, wq).then_inc(wqk_loaded, 16)
            sp.dma_start(wk_nat, wk).then_inc(wqk_loaded, 16)

            def load_ctx_piece(a):
                half, at = divmod(a * CTX_PIECE, PER)
                sp.dma_start(ctx_first[half][:, at:at + CTX_PIECE, :],
                             ctx_rows[a * CTX_PIECE:(a + 1) * CTX_PIECE].rearrange("j p c -> p j c"))\
                  .then_inc(ctx_first_loaded[a], 16)

            load_ctx_piece(0)
            load_ctx_piece(1)
            with nc.allow_non_contiguous_dma(reason="bias columns, 128 words each"):
                sp.dma_start(bq_col[:, :], bq.rearrange("(p a) -> p a", a=1)).then_inc(cols_loaded, 16)
                sp.dma_start(bk_col[:, :], bk.rearrange("(p a) -> p a", a=1)).then_inc(cols_loaded, 16)
                sp.dma_start(bab_col[0:S, :], ba.rearrange("(p a) -> p a", a=1)).then_inc(cols_loaded, 16)
                sp.dma_start(bab_col[S:P, :], bb.rearrange("(p a) -> p a", a=1)).then_inc(cols_loaded, 16)
            sp.dma_start(wab_nat[0:S, :], wa).then_inc(wab_loaded, 16)
            sp.dma_start(wab_nat[S:P, :], wb).then_inc(wab_loaded, 16)
            for copy in range(2):
                sp.dma_start(wout_4d[:, :, copy, :], wout.rearrange("(k p) s -> p k s", p=P)).then_inc(wout_loaded, 16)

            for a in range(2, CTX_FIRST // CTX_PIECE):
                sp.wait_ge(ctx_turned, CTX_PIECE * (a - 2) + 2)
                load_ctx_piece(a)

            def loads(sl):
                t = sl.tile(LOADS["ctx_load"], TILES, CTX_FIRST)
                if t:
                    if t.first >= CTX_FIRST + 2:
                        sp.wait_ge(ctx_turned, t.n - 1)
                    sp.dma_start(ctx_nat[:, t.odd, :], ctx_rows[t.n]).then_inc(ctx_loaded[t.odd], 16)
                if sl.tile(LOADS["x_first"], 1):
                    for n in range(2):
                        sp.dma_start(x_in[:, n, :], x_rows[n]).then_inc(x_loaded[n], 16)
                if sl.tile(LOADS["rows"], 1):
                    sp.dma_start(bout_all[:, :], bout.partition_broadcast(P)).then_inc(rows_loaded, 16)
                    sp.dma_start(fbias_all[:, :], fbias.partition_broadcast(P)).then_inc(rows_loaded, 16)
                t = sl.tile(LOADS["x_load"], TILES, 2)
                if t:
                    sp.wait_ge(x1_ready, t.n - 1)
                    sp.dma_start(x_in[:, t.odd, :], x_rows[t.n]).then_inc(x_loaded[t.odd], 16)
                t = sl.tile(LOADS["store"], TILES)
                if t:
                    sp.wait_ge(out_ready, t.n + 1)
                    sp.dma_start(out_rows[t.n], x_out[:, t.odd, :]).then_inc(stored[t.odd], 16)

            walk(sp, LOADS, TILES, loads, starts=dict(ctx_load=CTX_FIRST, x_load=2), counts=dict(x_first=1, rows=1))
            for odd in range(2):
                sp.wait_ge(stored[odd], 16 * TILES // 2)

        @block.gpsimd
        def _(gp):
            gp.memset(ident[:, :], 0.0).then_inc(gp_const_ready, 1)
            gp.memset(minus_half[:, :], -0.5).then_inc(gp_const_ready, 1)
            gp.wait_ge(gp_const_ready, 2)
            gp.affine_select(out=ident[:, :], in_=ident[:, :], compare_op=ALU.not_equal, fill=1.0, base=0,
                             pattern=[[-1, P]], channel_multiplier=1).then_inc(ident_ready, 1)

            def carry_wait():
                gp.sem_inc(wait_carrier, 1)

            def scales(k, t):
                gp.wait_ge(ln_stats[k], t.n + 1)
                if t.first:
                    gp.wait_ge(ln_done[k], t.n)
                carry_wait()
                gp.tensor_scalar(norm[:, k, 0:1], meanvar[:, k, 1:2], EPS, XN_SCALE ** -2, ALU.add, ALU.mult)\
                  .then_inc(ln_var[k], 1)
                gp.wait_ge(ln_var[k], t.n + 1)
                gp.tensor_tensor(norm[:, k, 1:2], norm[:, k, 0:1], minus_half[:, :], ALU.pow).then_inc(ln_rstd[k], 1)
                gp.wait_ge(ln_rstd[k], t.n + 1)
                carry_wait()
                gp.tensor_scalar(norm[:, k, 2:3], meanvar[:, k, 0:1], norm[:, k, 1:2], -1.0, ALU.mult, ALU.mult)\
                  .then_inc(ln_scales[k], 1)

            chunks = [(r, a) for r in range(R) for a in range(F_PARTS)]

            def add_factors(n):
                for r, a in chunks[:n]:
                    part = f_store[:, 2 * a:2 * a + 2, :]
                    if r:
                        gp.wait_ge(f_loaded[a], 16 * r)
                        gp.dma_start(part, f_rows[r, a], accum_op=ALU.add).then_inc(f_loaded[a], 16)
                    else:
                        gp.dma_start(part, f_rows[r, a]).then_inc(f_loaded[a], 16)
                del chunks[:n]

            gp.wait_ge(wqk_loaded, 32)
            gp.wait_ge(ctx_first_loaded[0], 16)

            def body(sl):
                add_factors(CHUNKS_AT_START.get(sl.first, 0))
                if sl.first == WOUT_MAX:
                    gp.wait_ge(w_rowmax, 2)
                    gp.partition_all_reduce(wout_s[:, 1:2], wout_s[:, 0:1], P, bass.bass_isa.ReduceOp.max)\
                      .then_inc(w_allmax, 1)
                t = sl.step("turn1", TILES)
                if t:
                    gp.wait_ge(ln_done[0], t.n + 1)
                    carry_wait()
                    gp.tensor_scalar(affine[:, 0:1], norm[:, 0, 1:2], 1.0 / XN_SCALE, 1.0, ALU.mult, ALU.add)
                    gp.tensor_scalar(affine[:, 1:2], norm[:, 0, 2:3], 1.0 / XN_SCALE, 0.0, ALU.mult, ALU.add)\
                      .then_inc(affine_done, 1)
                    gp.wait_ge(affine_done, 2 * t.n + 1)
                    carry_wait()
                    gp.tensor_scalar(x_in[:, t.odd, :], x_in[:, t.odd, :], affine[:, 0:1], affine[:, 1:2],
                                     ALU.mult, ALU.add).then_inc(affine_done, 1)
                    if t.first == 0:
                        gp.wait_ge(rows_loaded, 32)
                    gp.wait_ge(affine_done, 2 * t.n + 2)
                    gp.tensor_tensor(x_in[:, t.odd, :], x_in[:, t.odd, :], bout_all[:, :], ALU.add)\
                      .then_inc(res1_ready, 1)
                t = sl.tile(LEAD["scale_probs"], TILES)
                if t:
                    gp.wait_ge(inv_ready, t.n + 1)
                    carry_wait()
                    gp.tensor_scalar(probs[:, t.odd, :], probs[:, t.odd, :], row_inv[:, :], PROB_SCALE,
                                     ALU.mult, ALU.mult).then_inc(probs_ready, 1)
                add_factors(CHUNKS_AFTER_SCALING.get(sl.first, 0))
                t = sl.tile(LEAD["attend"], TILES)
                if t:
                    scales(2, t)
                t = sl.step("output", TILES)
                if t:
                    scales(1, t)
                if sl.first == 0:
                    add_factors(len(chunks))
                t = sl.step("ln1", TILES)
                if t:
                    scales(0, t)
                if sl.first == FACTORS_MAX:
                    gp.wait_ge(f_max, F_PARTS + 1)
                    gp.partition_all_reduce(f_s[:, 1:2], f_s[:, 0:1], P, bass.bass_isa.ReduceOp.max)\
                      .then_inc(f_allmax, 1)
                t = sl.tile(LEAD["attend"], TILES)
                if t:
                    gp.wait_ge(x2_ready, t.n + 1)
                    if t.first >= 2:
                        gp.wait_ge(stored[t.odd], 16 * t.half)
                    gp.tensor_tensor(x_out[:, t.odd, :], x_mid[:, t.odd, :], fbias_all[:, :], ALU.add)\
                      .then_inc(bias_added, 1)

            walk(gp, LEAD, TILES, body)

        @block.scalar
        def _(act):
            def high(out_ap, psum_ap):
                return nc.scalar.activation(out_ap, psum_ap, ACT.Copy)

            act.wait_ge(w_psum, 1)
            nc.scalar.copy(wqT[:, :], ps_t[:, 0:C]).then_inc(w_psum_read, 1)
            nc.scalar.copy(wkT[:, :], ps_t[:, C:2 * C]).then_inc(w_psum_read, 1)

            def normalise(k, t, src):
                act.wait_ge(ln_scales[k], t.n + 1)
                if k == 1:
                    act.wait_ge(xn_turned[0], t.n + 1)
                elif t.first:
                    act.wait_ge(xn_turned[1 if k == 0 else 2], t.n)
                nc.scalar.activation(xns[k][:, :], src, ACT.Identity, bias=norm[:, k, 2:3], scale=norm[:, k, 1:2])\
                  .then_inc(ln_done[k], 1)

            def split_factors(ks):
                for k in ks:
                    if k < KD - 2:
                        act.wait_ge(f_lo, KD - 2 - k)
                    nc.scalar.activation(f_part(k)[:, 0:D], f_store[:, k, :], ACT.Copy, scale=f_s[:, 3:4])\
                      .then_inc(f_hi, 1)

            def body(sl):
                ta = sl.tile(LEAD["attend"], TILES)

                def high_probs():
                    t = sl.tile(LEAD["probs"], TILES)
                    if t:
                        act.wait_ge(probs_turned, t.n + 1)
                        if t.first > PER:
                            act.wait_ge(attend_done, t.n - PER)
                        high(pt_hi[:, parity(t), :, bass.ds(in_batch(t), P)], blocks8(ps_probs(sl)[:, :]))\
                            .then_inc(pt_hi_ready, 1)

                def exponentials():
                    t = sl.tile(LEAD["energy"], TILES)
                    if t:
                        act.wait_ge(max_ready, t.n + 1)
                        if t.first >= 2:
                            act.wait_ge(probs_turned, t.n - 1)
                        if t.first:
                            act.wait_ge(inv_ready, t.n)
                        nc.scalar.activation(probs[:, t.odd, :], ps_energy(t)[:, :], ACT.Exp, bias=neg_max[:, :],
                                             accum_out=row_sum[:, :]).then_inc(exp_done, 1)

                if sl.first == -LEAD["energy"]:
                    act.wait_ge(w_psum, 2)
                    high(wabT[:, 0, :], ps_ffn[:, :]).then_inc(w_hi, 1)
                    act.wait_ge(w_psum, 3)
                    high(woutT[:, 0, :], ps_attend[:, :]).then_inc(w_hi, 1)
                if sl.first == FACTORS_SPLIT:
                    split_factors((KD - 3, KD - 4))
                t = sl.step("turn1", TILES)
                if t:
                    act.wait_ge(xn_turned[0], t.n + 1)
                    if t.first:
                        act.wait_ge(ab_done, t.n)
                    high(xn1T[:, 0, :], ps_xn1(t)[:, :]).then_inc(xn_hi[0], 1)
                if sl.first == FACTORS_SPLIT:
                    split_factors(reversed(range(KD - 4)))
                t = sl.step("gates", TILES)
                if t:
                    act.wait_ge(ab_done, t.n + 1)
                    if t.first == 0:
                        act.wait_ge(cols_loaded, 64)
                    else:
                        act.wait_ge(hs_ready, t.n)
                        act.wait_ge(carry_ready, t.n)
                    nc.scalar.activation(gate_a[:, :], ps_gates(t)[0:S, 0:P], ACT.Tanh, bias=bab_col[0:S, :],
                                         scale=wab_s[0:S, 4:5])
                    nc.scalar.activation(gate_b[:, :], ps_gates(t)[S:P, 0:P], ACT.Tanh, bias=bab_col[S:P, :],
                                         scale=wab_s[S:P, 4:5]).then_inc(gates_ready, 1)
                t = sl.tile(LEAD["turn_ctx"], TILES)
                if t:
                    act.wait_ge(ctx_turned, t.n + 1)
                    if t.first >= 2:
                        act.wait_ge(qk_done, t.n - 1)
                    nc.scalar.copy(ctxT[:, t.odd, :], ps_t[:, HALF:HALF + C]).then_inc(ctxT_ready, 1)
                if ta:
                    normalise(2, ta, x_mid[:, ta.odd, :])
                t = sl.tile(LEAD["project"], TILES)
                if t:
                    act.wait_ge(qk_done, t.n + 1)
                    if t.first == 0:
                        act.wait_ge(cols_loaded, 64)
                    if t.first > PER:
                        act.wait_ge(energy_done, t.n - PER)
                    for dst, at, bias in ((qT, 0, bq_col), (kT, P, bk_col)):
                        nc.scalar.activation(dst[:, parity(t), bass.ds(in_batch(t), P)], ps_project(t)[:, at:at + P],
                                             ACT.Identity, bias=bias[:, :]).then_inc(qk_ready, 1)
                if ta:
                    act.wait_ge(xn_turned[2], ta.n + 1)
                    if ta.first >= 2:
                        act.wait_ge(ffn_done, ta.n - 1)
                    high(xn3T[:, ta.odd, 0, :], ps_t[:, :]).then_inc(xn_hi[2], 1)
                t = sl.step("norm2", TILES)
                if t:
                    normalise(1, t, x_mid[:, t.odd, :])
                if sl.first < -1:
                    exponentials()
                high_probs()
                t = sl.step("turn2", TILES)
                if t:
                    act.wait_ge(xn_turned[1], t.n + 1)
                    if t.first:
                        act.wait_ge(attend_done, t.n)
                    high(xn2T[:, 0, :], ps_t[:, :]).then_inc(xn_hi[1], 1)
                t = sl.step("norm1", TILES)
                if t:
                    normalise(0, t, x_in[:, t.odd, :])
                if sl.first >= -1:
                    exponentials()
                if sl.first == FACTORS_MAX:
                    act.wait_ge(f_step, 4)
                    split_factors((KD - 1, KD - 2))

            walk(act, LEAD, TILES, body)

        @block.vector
        def _(dve):
            V = nc.vector
            V.memset(keep[:, :], 1.0).then_inc(const_ready, 1)
            dve.wait_ge(const_ready, 1)
            V.memset(keep[:, 0:TILES + 1:PER], 0.0)
            V.memset(carry[:, :], 0.0).then_inc(const_ready, 1)

            def power_scale(s, src, carried, step):
                V.tensor_scalar(s[:, 2:3], s[:, src:src + 1], 1e-30, None, ALU.max).then_inc(step, 1)
                dve.wait_ge(step, 1)
                V.tensor_scalar(s[:, 5:6].bitcast(I32), s[:, 2:3].bitcast(I32), 0x7F800000, None, ALU.bitwise_and)\
                 .then_inc(step, 1)
                dve.wait_ge(step, 2)
                V.tensor_scalar(s[:, 4:5], s[:, 5:6], carried / W_TOP, None, ALU.mult)
                V.tensor_scalar(s[:, 2:3], s[:, 5:6], 1.0 / W_TOP, None, ALU.mult).then_inc(step, 1)
                dve.wait_ge(step, 3)
                V.reciprocal(s[:, 3:4], s[:, 2:3]).then_inc(step, 1)
                dve.wait_ge(step, 4)

            dve.wait_ge(wab_loaded, 32)
            V.tensor_reduce(wab_s[:, 0:1], wab_nat, AX.X, ALU.max, apply_absolute_value=True)\
             .then_inc(w_rowmax, 1)
            dve.wait_ge(wout_loaded, 32)
            V.tensor_reduce(wout_s[:, 0:1], wout_nat, AX.X, ALU.max, apply_absolute_value=True)\
             .then_inc(w_rowmax, 1)
            dve.wait_ge(w_rowmax, 1)
            power_scale(wab_s, 0, 1.0 / XN_SCALE, wab_step)
            V.tensor_scalar(wab_nat, wab_nat, wab_s[:, 3:4], None, ALU.mult).then_inc(w_scaled, 1)
            dve.wait_ge(w_allmax, 1)
            power_scale(wout_s, 1, 1.0 / HS_SCALE, wout_step)
            V.tensor_scalar(wout_nat, wout_nat, wout_s[:, 3:4], None, ALU.mult).then_inc(w_scaled, 1)

            def low(out_ap, psum_ap, high_ap):
                return V.tensor_tensor(out_ap, psum_ap, high_ap, ALU.subtract)

            def moments(k, t, src):
                if t.first:
                    dve.wait_ge(ln_scales[k], t.n)
                for h in range(2):
                    V.bn_stats(stats[:, k, 6 * h:6 * h + 6], src[:, h * HALF:(h + 1) * HALF]).then_inc(ln_parts[k], 1)
                dve.wait_ge(ln_parts[k], 2 * t.n + 2)
                dve.sem_inc(wait_carrier, 1)
                V.bn_aggr(meanvar[:, k, :], stats[:, k, :]).then_inc(ln_stats[k], 1)

            def factors_max(parts):
                for a in parts:
                    dve.wait_ge(f_loaded[a], 16 * R)
                    V.tensor_reduce(f_most[:, a:a + 1], f_store[:, 2 * a:2 * a + 2, :], AX.XY, ALU.max,
                                    apply_absolute_value=True).then_inc(f_max, 1)

            def split_factors(ks):
                for k in ks:
                    dve.wait_ge(f_hi, KD - k)
                    V.scalar_tensor_tensor(f_part(k)[:, D:2 * D], f_store[:, k, :], f_s[:, 3:4],
                                           f_part(k)[:, 0:D], ALU.mult, ALU.subtract).then_inc(f_lo, 1)

            def ffn_result(t):
                dve.wait_ge(ffn_done, t.n + 1)
                dve.wait_ge(bias_added, t.n + 1)
                V.scalar_tensor_tensor(x_out[:, t.odd, :], ps_ffn[:, :], f_s[:, 4:5], x_out[:, t.odd, :],
                                       ALU.mult, ALU.add).then_inc(out_ready, 1)

            def body(sl):
                ta = sl.tile(LEAD["attend"], TILES)
                turn1, gates, output, turn2 = (sl.step(k, TILES) for k in ("turn1", "gates", "output", "turn2"))

                def energy_max():
                    t = sl.tile(LEAD["energy"], TILES)
                    if t:
                        dve.wait_ge(energy_done, t.n + 1)
                        if t.first:
                            dve.wait_ge(exp_done, t.n)
                        V.tensor_reduce(neg_max[:, :], ps_energy(t)[:, :], AX.X, ALU.max, negate=True)\
                         .then_inc(max_ready, 1)

                if sl.first == -LEAD["energy"]:
                    dve.wait_ge(w_hi, 1)
                    low(wabT[:, 1, :], ps_ffn[:, :], wabT[:, 0, :]).then_inc(w_psum_read, 1)
                    dve.wait_ge(w_hi, 2)
                    low(woutT[:, 1, :], ps_attend[:, :], woutT[:, 0, :]).then_inc(w_psum_read, 1)
                t = sl.tile(LEAD["scale_probs"], TILES)
                if t:
                    dve.wait_ge(exp_done, t.n + 1)
                    if t.first:
                        dve.wait_ge(probs_ready, t.n)
                    V.reciprocal(row_inv[:, :], row_sum[:, :]).then_inc(inv_ready, 1)
                t = sl.tile(LEAD["q_tile"], TILES)
                if t:
                    dve.wait_ge(qk_ready, 2 * t.n + 2)
                    if t.first >= 2:
                        dve.wait_ge(energy_done, t.n - 1)
                    V.tensor_copy(q_tile[:, t.odd, :], qT[:, parity(t), bass.ds(in_batch(t), P)])\
                     .then_inc(q_tile_ready, 1)
                if sl.first == FACTORS_MAX:
                    factors_max((0,))
                if sl.first == FACTORS_SPLIT:
                    split_factors(reversed(range(KD - 4, KD - 1)))
                if turn1:
                    dve.wait_ge(xn_hi[0], turn1.n + 1)
                    low(xn1T[:, 1, :], ps_xn1(turn1)[:, :], xn1T[:, 0, :]).then_inc(xnT_ready[0], 1)
                if sl.first == FACTORS_SPLIT:
                    split_factors(reversed(range(KD - 4)))
                if sl.first == FACTORS_MAX:
                    factors_max((1, 2))
                if ta:
                    dve.wait_ge(attend_done, ta.n + 1)
                    mid = x_mid[:, ta.odd, :]
                    V.scalar_tensor_tensor(mid, ps_attend[:, :], 1.0 / (XN_SCALE * PROB_SCALE), mid, ALU.mult, ALU.add)\
                     .then_inc(x2_ready, 1)
                if ta and ta.first == 0:
                    dve.wait_ge(x2_ready, ta.n + 1)
                    moments(2, ta, mid)
                if gates:
                    dve.wait_ge(gates_ready, gates.n + 1)
                    if gates.first == 0:
                        dve.wait_ge(const_ready, 2)
                    else:
                        dve.wait_ge(hs_ready, gates.n)
                        dve.wait_ge(carry_ready, gates.n)
                    V.tensor_tensor_scan(hs[:, :], gate_a[:, :], gate_b[:, :], carry[:, :], ALU.mult, ALU.add)\
                     .then_inc(scan_done, 1)
                    dve.wait_ge(scan_done, gates.n + 1)
                    if gates.first:
                        dve.wait_ge(mixer_done, gates.n)
                    V.tensor_scalar(hs_parts[0:S, :], hs[:, :], HS_SCALE, None, ALU.mult).then_inc(hs_hi, 1)
                    V.tensor_tensor(carry[:, :], hs[:, P - 1:P], keep[:, bass.ds(gates.n + 1, 1)], ALU.mult)\
                     .then_inc(carry_ready, 1)
                    dve.wait_ge(hs_hi, gates.n + 1)
                    V.scalar_tensor_tensor(hs_parts[S:P, :], hs[:, :], HS_SCALE, hs_parts[0:S, :],
                                           ALU.mult, ALU.subtract).then_inc(hs_ready, 1)
                if ta and ta.first:
                    dve.wait_ge(x2_ready, ta.n + 1)
                    moments(2, ta, mid)
                if output:
                    dve.wait_ge(mixer_done, output.n + 1)
                    dve.wait_ge(res1_ready, output.n + 1)
                    if output.first >= 2:
                        dve.wait_ge(ln_done[2], output.n - 1)
                        dve.wait_ge(bias_added, output.n - 1)
                    V.scalar_tensor_tensor(x_mid[:, output.odd, :], ps_c[:, :], wout_s[:, 4:5], x_in[:, output.odd, :],
                                           ALU.mult, ALU.add).then_inc(x1_ready, 1)
                    dve.wait_ge(x1_ready, output.n + 1)
                    moments(1, output, x_mid[:, output.odd, :])
                if sl.first == FACTORS_MAX:
                    factors_max((3,))
                    dve.wait_ge(f_max, F_PARTS)
                    V.tensor_reduce(f_s[:, 0:1], f_most[:, :], AX.X, ALU.max).then_inc(f_max, 1)
                if sl.first == FACTORS_SPLIT:
                    ffn_result(Tile(0, 0, 0))
                if ta:
                    dve.wait_ge(xn_hi[2], ta.n + 1)
                    low(xn3T[:, ta.odd, 1, :], ps_t[:, :], xn3T[:, ta.odd, 0, :]).then_inc(xnT_ready[2], 1)
                t = sl.step("ln1", TILES)
                if t:
                    dve.wait_ge(x_loaded[t.odd], 16 * t.half + 16)
                    moments(0, t, x_in[:, t.odd, :])
                if sl.first < -1:
                    energy_max()
                t = sl.tile(LEAD["probs"], TILES)
                if t:
                    dve.wait_ge(pt_hi_ready, t.n + 1)
                    cols = (slice(None), parity(t), slice(None), bass.ds(in_batch(t), P))
                    low(pt_lo[cols], blocks8(ps_probs(sl)[:, :]), pt_hi[cols]).then_inc(pt_ready, 1)
                if turn2:
                    dve.wait_ge(xn_hi[1], turn2.n + 1)
                    low(xn2T[:, 1, :], ps_t[:, :], xn2T[:, 0, :]).then_inc(xnT_ready[1], 1)
                t = sl.tile(LEAD["ffn"], TILES, 1)
                if t:
                    ffn_result(t)
                if sl.first >= -1:
                    energy_max()
                if sl.first == FACTORS_MAX:
                    dve.wait_ge(f_allmax, 1)
                    power_scale(f_s, 1, RSQRT_R / XN_SCALE, f_step)
                    split_factors((KD - 1,))

            walk(dve, LEAD, TILES, body)

        @block.tensor
        def _(pe):
            mm = nc.tensor.matmul

            def turn(ps, src, n):
                for k in range(n):
                    last = nc.tensor.transpose(ps[:, k * P:(k + 1) * P], src[:, k * P:(k + 1) * P], ident[:, :])
                return last

            pe.wait_ge(ident_ready, 1)
            pe.wait_ge(wqk_loaded, 32)
            turn(ps_t, x_out[:, 0, :], 2 * KC).then_inc(w_psum, 1)

            def products(ps, stat, mov, ks, starts=True, stops=True):
                for k in ks:
                    for n, (a, b) in enumerate(((0, 0), (0, 1), (1, 0))):
                        last = mm(ps, stat(k, a), mov(k, b), start=(starts and k == ks[0] and n == 0),
                                  stop=(stops and k == ks[-1] and n == 2))
                return last

            def body(sl):
                ta, tf = sl.tile(LEAD["attend"], TILES), sl.tile(LEAD["ffn"], TILES, 1)
                turn1, gates, output, turn2 = (sl.step(k, TILES) for k in ("turn1", "gates", "output", "turn2"))
                tt, tc, te, tp = (sl.tile(LEAD[k], TILES) for k in ("turn_ctx", "project", "energy", "probs"))
                if te and te.first == 0:
                    pe.wait_ge(w_scaled, 1)
                    turn(ps_ffn, wab_nat, KD).then_inc(w_psum, 1)
                    pe.wait_ge(w_scaled, 2)
                    turn(ps_attend, wout_nat, KD).then_inc(w_psum, 1)

                def turn_xn1():
                    pe.wait_ge(ln_done[0], turn1.n + 1)
                    if turn1.first:
                        pe.wait_ge(xnT_ready[1], turn1.n)
                    else:
                        pe.wait_ge(exp_done, te.n)
                    turn(ps_xn1(turn1), xn12, KD).then_inc(xn_turned[0], 1)

                def gate_products():
                    pe.wait_ge(xnT_ready[0], gates.n + 1)
                    if gates.first == 0:
                        pe.wait_ge(exp_done, te.n)
                    products(ps_gates(gates)[:, 0:P], lambda k, a: wabT[:, a, k * P:(k + 1) * P],
                             lambda k, b: xn1T[:, b, k * P:(k + 1) * P], range(KD)).then_inc(ab_done, 1)

                def attend(h):
                    cols = slice(h * HALF, (h + 1) * HALF)
                    return products(ps_attend[:, cols], lambda k, a: xn2T[:, a, k * P:(k + 1) * P],
                                    lambda k, b: (pt_hi, pt_lo)[b][:, parity(ta), k, cols], range(KD))

                def ffn(t, h, half):
                    first = 1 if t.first == 0 and h == 0 else 0
                    return products(ps_ffn[:, h * HALF:(h + 1) * HALF],
                                    lambda k, a: xn3T[:, t.odd, a, k * P:(k + 1) * P],
                                    lambda k, b: f_part(k)[:, b * D + h * HALF:b * D + (h + 1) * HALF],
                                    range(half * KD // 2, (half + 1) * KD // 2), half == first, half != first)

                def energies():
                    pe.wait_ge(q_tile_ready, te.n + 1)
                    pe.wait_ge(qk_ready, 2 * batch_tiles(te))
                    if te.first == 0:
                        pe.wait_ge(w_psum_read, 4)
                    elif te.first > LEAD["energy"]:
                        pe.wait_ge(exp_done, te.n)
                    elif te.first >= 2:
                        pe.wait_ge(exp_done, te.n - 1)
                    if sl.first == 1 - EARLY["turn1"]:
                        pe.wait_ge(xnT_ready[0], 1)
                    if sl.first == 1 - EARLY["gates"]:
                        pe.wait_ge(gates_ready, 1)
                    if output:
                        pe.wait_ge(x1_ready, output.n + 1)
                    if tp and ps_probs(sl) is ps_c:
                        pe.wait_ge(pt_ready, tp.n + 1)
                    for h in range(2):
                        last = mm(ps_energy(te)[:, h * HALF:(h + 1) * HALF], q_tile[:, te.odd, :],
                                  kT[:, parity(te), h * HALF:(h + 1) * HALF], start=True, stop=True)
                    last.then_inc(energy_done, 1)

                if ta:
                    pe.wait_ge(xnT_ready[1], ta.n + 1)
                    pe.wait_ge(pt_ready, batch_tiles(ta))
                    if ta.first:
                        pe.wait_ge(x2_ready, ta.n)
                    else:
                        pe.wait_ge(exp_done, LEAD["energy"] - 1)
                    attend(0)
                if turn1 and turn1.first:
                    turn_xn1()
                if ta:
                    attend(1).then_inc(attend_done, 1)
                if gates and gates.first:
                    gate_products()
                if tt:
                    if tt.first < CTX_FIRST:
                        source = ctx_first[tt.first // PER][:, tt.first % PER, :]
                        pe.wait_ge(ctx_first_loaded[tt.first // CTX_PIECE], 16)
                    else:
                        source = ctx_nat[:, tt.odd, :]
                        pe.wait_ge(ctx_loaded[tt.odd], 16 * (tt.half - CTX_FIRST // 2) + 16)
                    if tt.first:
                        pe.wait_ge(ctxT_ready, tt.n)
                    else:
                        pe.wait_ge(w_psum_read, 2)
                    turn(ps_t[:, HALF:2 * HALF], source, KC).then_inc(ctx_turned, 1)
                if sl.first == FACTORS_SPLIT:
                    pe.wait_ge(xnT_ready[2], 1)
                    pe.wait_ge(pt_ready, LEAD["probs"] + 2)
                    pe.wait_ge(f_lo, KD // 2)
                    ffn(Tile(0, 0, 0), 0, 1)
                    pe.wait_ge(f_lo, KD)
                    ffn(Tile(0, 0, 0), 0, 0)
                elif tf:
                    pe.wait_ge(xnT_ready[2], tf.n + 1)
                    pe.wait_ge(out_ready, tf.n)
                    ffn(tf, 0, 0)
                if output:
                    pe.wait_ge(hs_ready, output.n + 1)
                    if te:
                        pe.wait_ge(exp_done, te.n)
                    elif sl.tile(LEAD["scale_probs"], TILES):
                        pe.wait_ge(exp_done, TILES)
                    for h in range(2):
                        for part in range(2):
                            last = mm(ps_c[:, h * HALF:(h + 1) * HALF], hs_parts[:, :],
                                      woutT[:, part, h * HALF:(h + 1) * HALF], start=(part == 0), stop=(part == 1))
                    last.then_inc(mixer_done, 1)
                if tc:
                    pe.wait_ge(ctxT_ready, tc.n + 1)
                    if tc.first >= PER:
                        pe.wait_ge(qk_ready, 2 * tc.n)
                    elif tc.first >= 2:
                        pe.wait_ge(qk_ready, 2 * tc.n - 2)
                    else:
                        pe.wait_ge(w_psum_read, 2)
                    for at, w in ((0, wqT), (P, wkT)):
                        for k in range(KC):
                            last = mm(ps_project(tc)[:, at:at + P], w[:, k * P:(k + 1) * P],
                                      ctxT[:, tc.odd, k * P:(k + 1) * P], start=(k == 0), stop=(k == KC - 1))
                    last.then_inc(qk_done, 1)
                if sl.first == FACTORS_SPLIT:
                    ffn(Tile(0, 0, 0), 1, 0)
                    ffn(Tile(0, 0, 0), 1, 1).then_inc(ffn_done, 1)
                elif tf:
                    ffn(tf, 0, 1)
                if ta:
                    pe.wait_ge(ln_done[2], ta.n + 1)
                    if tc:
                        pe.wait_ge(qk_ready, 2 * tc.n + 2)
                    if tt:
                        pe.wait_ge(ctxT_ready, tt.n + 1)
                    turn(ps_t, xn3, KD).then_inc(xn_turned[2], 1)
                if te and sl.first < -1:
                    energies()
                if tp:
                    pe.wait_ge(probs_ready, tp.n + 1)
                    if ps_probs(sl) is ps_c:
                        if output:
                            pe.wait_ge(x1_ready, output.n + 1)
                    elif tp.first:
                        pe.wait_ge(pt_ready, tp.n)
                    else:
                        pe.wait_ge(w_psum_read, 4)
                    turn(ps_probs(sl), probs[:, tp.odd, :], KD).then_inc(probs_turned, 1)
                if turn1 and turn1.first == 0:
                    turn_xn1()
                if gates and gates.first == 0:
                    gate_products()
                if sl.first == FACTORS_SPLIT:
                    pe.wait_ge(xnT_ready[2], tf.n + 1)
                    pe.wait_ge(out_ready, tf.n)
                    ffn(tf, 0, 0)
                    ffn(tf, 0, 1)
                elif tf:
                    ffn(tf, 1, 0)
                if turn2:
                    pe.wait_ge(ln_done[1], turn2.n + 1)
                    if ta:
                        pe.wait_ge(xnT_ready[2], ta.n + 1)
                    else:
                        pe.wait_ge(qk_ready, 2 * tc.n + 2)
                        pe.wait_ge(ctxT_ready, tt.n + 1)
                    turn(ps_t, xn12, KD).then_inc(xn_turned[1], 1)
                if sl.first == FACTORS_SPLIT:
                    ffn(tf, 1, 0)
                if tf:
                    ffn(tf, 1, 1).then_inc(ffn_done, 1)
                if te and sl.first >= -1:
                    energies()

            walk(pe, LEAD, TILES, body)


_INS = ['x', 'ctx_1024', 'L0_attn_Wa', 'L0_attn_ba', 'L0_attn_Wb', 'L0_attn_bb', 'L0_attn_Wout', 'L0_attn_bout',
        'L0_xattn_Wq', 'L0_xattn_bq', 'L0_xattn_Wk', 'L0_xattn_bk', 'L0_ffn_factors', 'L0_ffn_bias']


def kernel(**inputs):
    import numpy as np
    import concourse.bacc as bacc
    from concourse.bass_utils import run_bass_kernel_spmd

    nc = bacc.Bacc("TRN2", target_bir_lowering=False, num_devices=1)
    arrays, args = {}, []
    for name in _INS:
        a = np.ascontiguousarray(inputs[name])
        arrays[f"in_{name}"] = a
        args.append(nc.dram_tensor(f"in_{name}", a.shape, mybir.dt.from_np(a.dtype), kind="ExternalInput").ap())
    shape = inputs['x'].shape
    args.append(nc.dram_tensor("out_0", shape, F32, kind="ExternalOutput").ap())
    decoder_kernel(nc, *args)
    r = run_bass_kernel_spmd(nc, [arrays], core_ids=[0])
    return r.results[0]["out_0"]
```
